# Optimizing a Trainium2 kernel written in Bass

```python
import numpy as np
import jax
import jax.numpy as jnp

def _softmax(x, axis=-1):
    return jax.nn.softmax(x, axis=axis)

def _gelu(x):
    return jax.nn.gelu(x, approximate=True)

def _silu(x):
    return jax.nn.silu(x)

def _sigmoid(x):
    return jax.nn.sigmoid(x)

def _layernorm(x, axis=-1, eps=1e-05):
    m = jnp.mean(x, axis=axis, keepdims=True)
    v = jnp.var(x, axis=axis, keepdims=True)
    return (x - m) / jnp.sqrt(v + eps)

def _scatter_add(tgt, idx, src, axis=0):
    return tgt.at[idx].add(src)

def _segment_sum(src, seg, n):
    return jax.ops.segment_sum(src, seg, n)
kernel_name = 'mk_prb_d1_jaxref_r8_bd78e9'

def setup_inputs(seed: int=0):
    np.random.seed(seed)
    _w = jnp.asarray

    def _L0_attn_setup():
        import jax, jax.numpy as jnp
        import numpy as np
        D_MODEL = 256
        N_QUERY = 4
        N_HEAD = 8
        D_HEAD = D_MODEL // (N_QUERY * N_HEAD)
        D_KV = D_HEAD * N_HEAD
        BATCH, SEQ = (2, 256)
        key = jax.random.key(seed)
        ks = jax.random.split(key, 5)
        w_scale = 1.0 / np.sqrt(D_MODEL).astype(np.float32)
        x = jax.random.normal(ks[0], (BATCH, SEQ, D_MODEL), jnp.float32)
        Wq = jax.random.normal(ks[1], (D_MODEL, D_MODEL), jnp.float32) * w_scale
        Wk = jax.random.normal(ks[2], (D_KV, D_MODEL), jnp.float32) * w_scale
        Wv = jax.random.normal(ks[3], (D_KV, D_MODEL), jnp.float32) * w_scale
        memory = jax.random.normal(ks[4], (D_KV, D_KV), jnp.float32) * 0.02
        memory_norm = jnp.ones((D_KV, 1), jnp.float32)
        memory_weight = jnp.ones((1,), jnp.float32)
        return dict(x=x, Wq=Wq, Wk=Wk, Wv=Wv, memory=memory, memory_norm=memory_norm, memory_weight=memory_weight)
    _L0_attn_in = _L0_attn_setup()

    def _L0_ffn_setup():
        import jax, jax.numpy as jnp
        import numpy as np
        B, S, H = (4, 256, 256)
        INTER = 512
        E = 8
        TOPK = 2
        SHARED_I = INTER * 2

        def moe_forward(hidden_states, router_w, w1, w2, w_gate, w_up, w_down):
            b, s, h = hidden_states.shape
            x = hidden_states.reshape(-1, h)
            T = x.shape[0]
            logits = x @ router_w
            top_logits, top_indices = jax.lax.top_k(logits, TOPK)
            scores = jax.nn.softmax(top_logits, axis=-1)
            flat_idx = top_indices.reshape(-1)
            sorted_pos = jnp.argsort(flat_idx, stable=True)
            permuted = x[sorted_pos // TOPK]
            expert_ids = flat_idx[sorted_pos]
            out = jnp.zeros((T * TOPK, h), x.dtype)
            for e in range(E):
                mask = (expert_ids == e)[:, None]
                f1 = permuted * mask @ w1[e]
                g, u = jnp.split(f1, 2, axis=-1)
                act = jax.nn.silu(g) * u
                out = out + jnp.where(mask, act @ w2[e], 0.0)
            unperm = jnp.zeros_like(out).at[sorted_pos].set(out)
            combined = (unperm.reshape(T, TOPK, h) * scores[..., None]).sum(axis=1)
            shared = jax.nn.silu(x @ w_gate) * (x @ w_up) @ w_down
            return (combined + shared).reshape(b, s, h)
        key = jax.random.key(seed)
        ks = jax.random.split(key, 7)
        s = 0.02
        return {'hidden_states': jax.random.normal(ks[0], (B, S, H), jnp.float32), 'router_w': jax.random.normal(ks[1], (H, E), jnp.float32) * s, 'w1': jax.random.normal(ks[2], (E, H, 2 * INTER), jnp.float32) * s, 'w2': jax.random.normal(ks[3], (E, INTER, H), jnp.float32) * s, 'w_gate': jax.random.normal(ks[4], (H, SHARED_I), jnp.float32) * s, 'w_up': jax.random.normal(ks[5], (H, SHARED_I), jnp.float32) * s, 'w_down': jax.random.normal(ks[6], (SHARED_I, H), jnp.float32) * s}
    _L0_ffn_in = _L0_ffn_setup()
    _d = {'L0_attn_x': _L0_attn_in['x'], 'L0_attn_Wq': _L0_attn_in['Wq'], 'L0_attn_Wk': _L0_attn_in['Wk'], 'L0_attn_Wv': _L0_attn_in['Wv'], 'L0_attn_memory': _L0_attn_in['memory'], 'L0_attn_memory_norm': _L0_attn_in['memory_norm'], 'L0_attn_memory_weight': _L0_attn_in['memory_weight'], 'L0_ffn_router_w': _L0_ffn_in['router_w'], 'L0_ffn_w1': _L0_ffn_in['w1'], 'L0_ffn_w2': _L0_ffn_in['w2'], 'L0_ffn_w_gate': _L0_ffn_in['w_gate'], 'L0_ffn_w_up': _L0_ffn_in['w_up'], 'L0_ffn_w_down': _L0_ffn_in['w_down']}
    _x0 = _d['L0_attn_x']
    _d['L0_attn_x'] = jax.random.normal(jax.random.fold_in(jax.random.key(seed), 1), (4, 512, 256), dtype=_x0.dtype)
    del _x0
    return _d

def reference(L0_attn_x, L0_attn_Wq, L0_attn_Wk, L0_attn_Wv, L0_attn_memory, L0_attn_memory_norm, L0_attn_memory_weight, L0_ffn_router_w, L0_ffn_w1, L0_ffn_w2, L0_ffn_w_gate, L0_ffn_w_up, L0_ffn_w_down):

    def _L0_attn_ref(x, Wq, Wk, Wv, memory, memory_norm, memory_weight):
        import jax, jax.numpy as jnp
        import numpy as np
        D_MODEL = 256
        N_QUERY = 4
        N_HEAD = 8
        D_HEAD = D_MODEL // (N_QUERY * N_HEAD)
        D_KV = D_HEAD * N_HEAD
        BATCH, SEQ = (2, 256)
        b, s, d = x.shape
        q = x @ Wq.T
        k = x @ Wk.T
        v = x @ Wv.T
        qh = q.reshape(b, s, N_QUERY, N_HEAD, D_HEAD)
        kh = k.reshape(b, s, N_HEAD, D_HEAD)
        vh = v.reshape(b, s, N_HEAD, D_HEAD)
        scale = np.float32(1.0 / np.sqrt(np.float32(D_HEAD)))
        scores = jnp.einsum('bsqhd,bthd->bqhst', qh, kh) * scale
        probs = jax.nn.softmax(scores, axis=-1)
        a_dot = jnp.einsum('bqhst,bthd->bsqhd', probs, vh)
        a_dot = a_dot.reshape(b, s, N_QUERY * N_HEAD, D_HEAD)
        sigma_q = jax.nn.elu(q.reshape(b, s, N_QUERY, D_KV))
        a_mem = sigma_q @ memory / (sigma_q @ memory_norm)
        a_mem = a_mem.reshape(b, s, N_QUERY * N_HEAD, D_HEAD)
        w = jax.nn.sigmoid(memory_weight)
        out = a_dot * (1.0 - w) + a_mem * w
        return out.reshape(b, s, D_MODEL)

    def _L0_ffn_ref(hidden_states, router_w, w1, w2, w_gate, w_up, w_down):
        import jax, jax.numpy as jnp
        import numpy as np
        B, S, H = (4, 256, 256)
        INTER = 512
        E = 8
        TOPK = 2
        SHARED_I = INTER * 2

        def moe_forward(hidden_states, router_w, w1, w2, w_gate, w_up, w_down):
            b, s, h = hidden_states.shape
            x = hidden_states.reshape(-1, h)
            T = x.shape[0]
            logits = x @ router_w
            top_logits, top_indices = jax.lax.top_k(logits, TOPK)
            scores = jax.nn.softmax(top_logits, axis=-1)
            flat_idx = top_indices.reshape(-1)
            sorted_pos = jnp.argsort(flat_idx, stable=True)
            permuted = x[sorted_pos // TOPK]
            expert_ids = flat_idx[sorted_pos]
            out = jnp.zeros((T * TOPK, h), x.dtype)
            for e in range(E):
                mask = (expert_ids == e)[:, None]
                f1 = permuted * mask @ w1[e]
                g, u = jnp.split(f1, 2, axis=-1)
                act = jax.nn.silu(g) * u
                out = out + jnp.where(mask, act @ w2[e], 0.0)
            unperm = jnp.zeros_like(out).at[sorted_pos].set(out)
            combined = (unperm.reshape(T, TOPK, h) * scores[..., None]).sum(axis=1)
            shared = jax.nn.silu(x @ w_gate) * (x @ w_up) @ w_down
            return (combined + shared).reshape(b, s, h)
        return moe_forward(hidden_states, router_w, w1, w2, w_gate, w_up, w_down)
    x = L0_attn_x
    xn = _layernorm(x, axis=-1)
    x = x + _L0_attn_ref(xn, L0_attn_Wq, L0_attn_Wk, L0_attn_Wv, L0_attn_memory, L0_attn_memory_norm, L0_attn_memory_weight) + _L0_ffn_ref(xn, L0_ffn_router_w, L0_ffn_w1, L0_ffn_w2, L0_ffn_w_gate, L0_ffn_w_up, L0_ffn_w_down)
    return x

_drawn_inputs = setup_inputs


def setup_inputs(seed=0):
    import zlib

    import numpy as np

    out = dict(_drawn_inputs(seed))
    spreads = {'L0_attn_memory_norm': (1.0, 0.2)}
    factors = {'L0_ffn_router_w': 4.749,
     'L0_ffn_w1': 4.095,
     'L0_ffn_w2': 4.101,
     'L0_attn_Wk': 4.227,
     'L0_attn_Wv': 3.893,
     'L0_ffn_w_gate': 3.361,
     'L0_ffn_w_up': 3.315,
     'L0_ffn_w_down': 3.316}
    for name, (base, spread) in spreads.items():
        noise = np.random.default_rng([zlib.crc32(name.encode()), seed]).standard_normal(out[name].shape)
        drawn = base * np.exp(spread * noise) if base else spread * noise
        out[name] = jnp.asarray(drawn.astype(out[name].dtype))
    for name, factor in factors.items():
        out[name] = (out[name] * factor).astype(out[name].dtype)
    return out
```

```python
from contextlib import ExitStack

import numpy as np

import concourse.bass as bass
from concourse import mybir

F32 = mybir.dt.float32
BF16 = mybir.dt.bfloat16
I32 = mybir.dt.int32
U32 = mybir.dt.uint32
ALU = mybir.AluOpType
ACT = mybir.ActivationFunctionType
X_AXIS = mybir.AxisListType.X

P = 128


def wait(eng, sem, value):
    if isinstance(value, int) and value <= 0:
        return
    eng.wait_ge(sem, value)


def build(nc, x, wqT, wkT, wvT, memory, memory_norm, memory_weight, router_w, w1, w2, w_gate, w_up, w_down, out):
    BATCH, SEQ, D = x.shape
    T = BATCH * SEQ
    NT = T // P
    KD = D // P
    DKV = wkT.shape[1]
    DH = 8
    H = DKV // DH
    G = D // DKV
    ST = SEQ // P
    STEPS = BATCH * H
    E, _, F2 = w1.shape
    F = F2 // 2
    FS = w_gate.shape[1]
    TOPK = 2
    TILES = (T * TOPK + E * (P - 1)) // P
    SLOTS = TILES * P
    SCALE = float(np.float32(1.0 / np.sqrt(np.float32(DH))))
    EPS = 1e-5
    Q_PART = (0, 0, 1, 1, 0, 2)
    K_PART = (0, 1, 0, 1, 2, 0)
    NC = len(Q_PART)
    R = NC * DH
    RM = R + 3
    MEMW = DKV + 1
    assert (D, DKV, H, G, ST, E, F, FS, TILES) == (256, 64, 8, 4, 4, 8, 512, 1024, 39)

    q_stacks = nc.dram_tensor("q_stacks", [G, H, R, T], BF16, kind="Internal").ap()
    k_stacks = nc.dram_tensor("k_stacks", [H, R, T], BF16, kind="Internal").ap()
    slot_x = nc.dram_tensor("slot_x", [SLOTS, D], F32, kind="Internal").ap()
    slot_y = nc.dram_tensor("slot_y", [SLOTS, D], F32, kind="Internal").ap()

    x_rows = x.rearrange("b s d -> (b s) d")
    out_rows = out.rearrange("b s d -> (b s) d")

    with ExitStack() as ctx:
        def sb(name, shape, dt=F32):
            return ctx.enter_context(nc.sbuf_tensor(name, shape, dt))

        def sem(name):
            return ctx.enter_context(nc.semaphore(name))

        ps = ctx.enter_context(nc.psum_tensor("ps", [P, 8, 512], F32))

        acc = sb("acc", [P, NT, D])
        xn = sb("xn", [P, NT, D])
        xnT = sb("xnT", [P, KD, T])
        big = sb("big", [P, 24576])
        att = sb("att", [P, 9216])
        o_sb = sb("o_sb", [P, 2, 512])
        v_all = sb("v_all", [P, NT, DKV])
        v_head = sb("v_head", [P, 2, ST, 32])
        ident = sb("ident", [P, P])
        before = sb("before", [P, P], BF16)
        ones = sb("ones", [P, 512], BF16)
        zeros = sb("zeros", [P, D])
        mem_w = sb("mem_w", [P, 2 * MEMW])
        router = sb("router", [P, KD, E])
        mixw = sb("mixw", [P, 4])
        stats = sb("stats", [P, NT, 6])
        meanvar = sb("meanvar", [P, NT, 2])
        sd = sb("sd", [P, NT])
        rstd = sb("rstd", [P, NT])
        logits = sb("logits", [P, NT, E])
        top = sb("top", [P, NT, 8])
        topi = sb("topi", [P, NT, 8], U32)
        choice = sb("choice", [P, TOPK, NT])
        score = sb("score", [P, TOPK, NT])
        iota_e = sb("iota_e", [P, E])
        iota_t = sb("iota_t", [P, TILES])
        full_at = sb("full_at", [P, NT])
        onehot = sb("onehot", [P, TOPK * NT, E], BF16)
        tiles_e = sb("tiles_e", [P, E])
        cum_a = sb("cum_a", [P, E])
        cum_b = sb("cum_b", [P, E])
        slot_f = sb("slot_f", [P, TOPK * NT])
        slot = sb("slot", [P, TOPK * NT], U32)
        expert_f = sb("expert_f", [P, TILES])
        expert = sb("expert", [P, TILES], I32)
        mden = sb("mden", [P, 2, G])
        smax = sb("smax", [P, 2, 16])
        negm = sb("negm", [16, 2, P])
        negr = sb("negr", [16, 2, P])
        m_parts = sb("m_parts", [16, 2, 3, P], BF16)
        rden = sb("rden", [P, 2, 16])
        otmp = sb("otmp", [P, 2, 16, DH])

        rank, total, run_a, run_b = [att[:, 256 * n:256 * (n + 1)].rearrange("p (w e) -> p w e", e=E)
                                     for n in range(4)]
        gt = att[:, 1024:1152].rearrange("p (e c) -> p e c", e=E)
        le = att[:, 1152:1152 + TILES * E].rearrange("p (j e) -> p j e", e=E)
        mtmp = att[:, 1536:1536 + 2 * D].rearrange("p (a d) -> p a d", a=2)
        qf = big[:, 0:4096].rearrange("p (m t) -> p m t", m=KD)
        qr = big[:, 4096:8192].rearrange("p (m t) -> p m t", m=KD)
        qc = [big[:, 8192 + 2048 * n:8192 + 2048 * (n + 1)].bitcast(BF16).rearrange("p (m t) -> p m t", m=KD)
              for n in range(3)]
        kf = big[0:DKV, 14336:16384]
        kr = big[0:DKV, 16384:18432]
        kc = [big[0:DKV, 18432 + 1024 * n:18432 + 1024 * (n + 1)].bitcast(BF16) for n in range(3)]
        wq_sb = big[:, 21504:22016].rearrange("p (k n) -> p k n", k=KD)
        wk_sb = big[:, 22016:22144].rearrange("p (k n) -> p k n", k=KD)
        wv_sb = big[:, 22144:22272].rearrange("p (k n) -> p k n", k=KD)
        w1_sb = big[:, 0:16384].rearrange("p (e k n) -> p e k n", e=E, k=KD)
        w2_sb = big[:, 16384:24576].rearrange("p (e k n) -> p e k n", e=E, k=F // P)
        probs = att[:, 0:4096].rearrange("p (a g s) -> p a g s", a=2, g=G)
        q_st = [att[:, 4096 + 1024 * n:5120 + 1024 * n].bitcast(BF16).rearrange("p (g s) -> p g s", g=G)
                for n in range(4)]
        k_st = [att[:, 8192 + 256 * n:8448 + 256 * n].bitcast(BF16) for n in range(4)]
        wg_sb = att[:, 0:2048].rearrange("p (k n) -> p k n", k=KD)
        wu_sb = att[:, 2048:4096].rearrange("p (k n) -> p k n", k=KD)
        wd_sb = att[:, 4096:6144].rearrange("p (k n) -> p k n", k=FS // P)
        sh_silu = big[:, 0:1024].rearrange("p (a n) -> p a n", a=2)
        sh_h = big[:, 1024:2048].rearrange("p (a n) -> p a n", a=2)
        xnf = xn[:, :, :].rearrange("p c d -> p (c d)")
        e_x = o_sb[:, :, 0:D]
        e_xT = xnf[:, 0:512].rearrange("p (a k n) -> p a k n", a=2, k=KD)
        e_silu = xnf[:, 512:1536].rearrange("p (a n) -> p a n", a=2)
        e_h = xnf[:, 1536:2560].rearrange("p (a n) -> p a n", a=2)
        e_hT = xnf[:, 2560:3584].rearrange("p (a k n) -> p a k n", a=2, k=F // P)
        e_y = xnf[:, 3584:4096].rearrange("p (a n) -> p a n", a=2)
        gath = xnf[:, 0:2048].rearrange("p (a n) -> p a n", a=8)

        x_loaded = [sem(f"x_loaded{n}") for n in range(4)]
        proj_loaded = sem("proj_loaded")
        small_loaded = sem("small_loaded")
        mem_loaded = sem("mem_loaded")
        mem_zero = sem("mem_zero")
        ident_zero = sem("ident_zero")
        ident_ready = sem("ident_ready")
        consts_ready = sem("consts_ready")
        slots_cleared = sem("slots_cleared")
        dve_step = sem("dve_step")
        act_step = sem("act_step")
        pool_step = sem("pool_step")
        var_ready = sem("var_ready")
        sd_ready = sem("sd_ready")
        xn_ready = sem("xn_ready")
        xT_in_psum = sem("xT_in_psum")
        xT_even = sem("xT_even")
        xT_odd = sem("xT_odd")
        logits_in_psum = sem("logits_in_psum")
        v_in_psum = sem("v_in_psum")
        v_copied = sem("v_copied")
        qk_in_psum = sem("qk_in_psum")
        qk_copied = sem("qk_copied")
        part_hi = sem("part_hi")
        residual = sem("residual")
        part_mid = sem("part_mid")
        part_lo = sem("part_lo")
        stacks_written = sem("stacks_written")
        q_min = sem("q_min")
        q_elu_parts = sem("q_elu_parts")
        sigma_ready = sem("sigma_ready")
        mem_in_psum = sem("mem_in_psum")
        mem_used = sem("mem_used")
        mix_exp = sem("mix_exp")
        gap_ready = sem("gap_ready")
        gap_exp = sem("gap_exp")
        onehot_ready = sem("onehot_ready")
        ranks_in_psum = sem("ranks_in_psum")
        routed = sem("routed")
        scattered = sem("scattered")

        ones_rows = sem("ones_rows")
        stack_loaded = [sem(f"stack_loaded{n}") for n in range(4)]
        m_loaded = [sem(f"m_loaded{n}") for n in range(2)]
        a_ready = sem("a_ready")
        max_done = sem("max_done")
        maxT_in_psum = sem("maxT_in_psum")
        negm_ready = sem("negm_ready")
        m_hi = sem("m_hi")
        m_res = sem("m_res")
        m_mid = sem("m_mid")
        m_ready = sem("m_ready")
        scores_ready = sem("scores_ready")
        probs_ready = sem("probs_ready")
        v_head_ready = sem("v_head_ready")
        pv_done = sem("pv_done")
        o_copied = sem("o_copied")
        oT_in_psum = sem("oT_in_psum")
        rden_ready = sem("rden_ready")
        o_ready = sem("o_ready")
        o_added = sem("o_added")

        w12_loaded = sem("w12_loaded")
        ex_loaded = [sem(f"ex_loaded{n}") for n in range(2)]
        exT_in_psum = sem("exT_in_psum")
        exT_ready = sem("exT_ready")
        up_done = sem("up_done")
        silu_done = sem("silu_done")
        h_ready = sem("h_ready")
        hT_in_psum = sem("hT_in_psum")
        hT_ready = sem("hT_ready")
        y_in_psum = sem("y_in_psum")
        y_ready = sem("y_ready")
        y_stored = [sem(f"y_stored{n}") for n in range(2)]
        shw_loaded = sem("shw_loaded")

        gathered = sem("gathered")
        s_up = sem("s_up")
        s_silu = sem("s_silu")
        s_h = sem("s_h")
        s_hused = sem("s_hused")
        s_down = sem("s_down")
        s_add = sem("s_add")
        s_mix = sem("s_mix")
        stored = sem("stored")

        block = ctx.enter_context(nc.Block())
        NF = FS // P

        def live(j):
            return not isinstance(j, int) or 0 <= j < TILES

        def over_tiles(eng, tile):
            for j in range(4):
                tile(j, j // 2, j % 2)
            with eng.Fori(2, TILES // 2 - 1) as pair:
                for a in range(2):
                    tile(pair * 2 + a, pair, a)
            for j in range(TILES // 2 * 2 - 2, TILES + 2):
                tile(j, j // 2, j % 2)

        NLOOP = STEPS // 4

        @block.sync
        def _(sp):
            for n in range(4):
                sp.dma_start(acc[:, 4 * n:4 * n + 4, :],
                             x_rows[512 * n:512 * (n + 1), :].rearrange("(c p) d -> p c d", p=P))\
                  .then_inc(x_loaded[n], 16)
            sp.dma_start(router[:, :, :], router_w.rearrange("(k p) n -> p k n", p=P)).then_inc(proj_loaded, 16)
            sp.dma_start(wv_sb, wvT.rearrange("(k p) n -> p k n", p=P)).then_inc(proj_loaded, 16)
            sp.dma_start(wk_sb, wkT.rearrange("(k p) n -> p k n", p=P)).then_inc(proj_loaded, 16)
            sp.dma_start(wq_sb, wqT.rearrange("(k p) n -> p k n", p=P)).then_inc(proj_loaded, 16)
            sp.dma_start(mixw[:, 0:1], memory_weight.partition_broadcast(P)).then_inc(small_loaded, 16)
            sp.wait_ge(mem_zero, 1)
            for a in range(2):
                sp.dma_start(mem_w[DKV * a:DKV * (a + 1), MEMW * a:MEMW * a + DKV], memory).then_inc(mem_loaded, 16)
                sp.dma_start(mem_w[DKV * a:DKV * (a + 1), MEMW * a + DKV:MEMW * (a + 1)], memory_norm)\
                  .then_inc(mem_loaded, 16)
            sp.wait_ge(consts_ready, 1)
            sp.dma_start(slot_x.rearrange("(j p) d -> p j d", p=P),
                         zeros[:, :].unsqueeze(1).to_broadcast([P, TILES, D])).then_inc(slots_cleared, 16)
            for n in range(4):
                sp.dma_start(k_st[n][R:RM, :], ones[0:3, :]).then_inc(ones_rows, 16)
            for part, done in ((0, part_hi), (1, part_mid), (2, part_lo)):
                sp.wait_ge(done, 1)
                for c in range(NC):
                    if K_PART[c] == part:
                        sp.dma_start(k_stacks[:, DH * c:DH * (c + 1), :], kc[part][:, :]).then_inc(stacks_written, 16)
            for part, done in ((0, part_hi), (1, part_mid), (2, part_lo)):
                sp.wait_ge(done, 2)
                for c in range(NC):
                    if Q_PART[c] == part:
                        for m in range(KD):
                            sp.dma_start(q_stacks[2 * m:2 * m + 2, :, DH * c:DH * (c + 1), :], qc[part][:, m, :])\
                              .then_inc(stacks_written, 16)
            sp.wait_ge(stacks_written, 16 * NC * (1 + KD))

            def load_stack(b, h, n):
                sp.dma_start(q_st[n][0:R, :, :],
                             q_stacks[:, bass.ds(h, 1), :, bass.ds(b * SEQ, SEQ)].rearrange("g o r t -> r (o g) t"))\
                  .then_inc(stack_loaded[n], 16)
                sp.dma_start(k_st[n][0:R, :],
                             k_stacks[bass.ds(h, 1), :, bass.ds(b * SEQ, SEQ)].rearrange("o r t -> r (o t)"))\
                  .then_inc(stack_loaded[n], 16)

            def m_rows(i, s):
                sp.wait_ge(m_ready, i + 1)
                for c in range(3):
                    sp.dma_start(q_st[s % 4][R + c:R + c + 1, :, :].rearrange("o g s -> o (g s)"),
                                 m_parts[0:16, s % 2, c, :]).then_inc(m_loaded[s % 2], 16)

            for n in range(3):
                load_stack(0, n, n)
            if True:
                def steps(b, h0, last):
                    for s in range(4):
                        i = b * H + (h0 + s)
                        m_rows(i, s)
                        if last and s > 0:
                            continue
                        wait(sp, scores_ready, i * 16)
                        if h0 == 4 and s > 0:
                            load_stack(b + 1, s - 1, (s + 3) % 4)
                        else:
                            load_stack(b, h0 + s + 3, (s + 3) % 4)
                steps(0, 0, False)
                steps(0, 4, False)
                with sp.Fori(1, BATCH - 1) as b:
                    steps(b, 0, False)
                    steps(b, 4, False)
                steps(BATCH - 1, 0, False)
                steps(BATCH - 1, 4, True)

            sp.wait_ge(pv_done, ST * STEPS)
            sp.dma_start(wg_sb, w_gate.rearrange("(k p) n -> p k n", p=P)).then_inc(shw_loaded, 16)
            sp.dma_start(wu_sb, w_up.rearrange("(k p) n -> p k n", p=P)).then_inc(shw_loaded, 16)
            sp.dma_start(wd_sb, w_down.rearrange("(k p) n -> p k n", p=P)).then_inc(shw_loaded, 16)

            sp.wait_ge(scattered, 16 * TOPK * NT)
            sp.wait_ge(oT_in_psum, STEPS)

            def load_x(j, a):
                wait(sp, exT_in_psum, j - 1)
                sp.dma_start(e_x[:, a, :], slot_x[bass.ds(j * P, P), :]).then_inc(ex_loaded[a], 16)

            def store_y(j, a):
                sp.wait_ge(y_ready, j + 1)
                sp.dma_start(slot_y[bass.ds(j * P, P), :], e_y[:, a, :]).then_inc(y_stored[a], 16)

            def tile(j, pair, a):
                if live(j + 2):
                    load_x(j + 2, a)
                if live(j - 2):
                    store_y(j - 2, a)

            load_x(0, 0)
            load_x(1, 1)
            over_tiles(sp, tile)

            with sp.Fori(0, 4) as n:
                sp.wait_ge(s_mix, (n + 1) * 8)
                sp.dma_start(out_rows[bass.ds(n * 512, 512), :].rearrange("(c p) d -> p c d", p=P),
                             acc[:, bass.ds(n * 4, 4), :]).then_inc(stored, 16)
            sp.wait_ge(stored, 64)

        @block.gpsimd
        def _(pool):
            count = [0]

            def link(ins):
                count[0] += 1
                ins.then_inc(pool_step, 1)
                pool.wait_ge(pool_step, count[0])

            pool.memset(ident[:, :], 0.0).then_inc(ident_zero, 1)
            pool.wait_ge(ident_zero, 1)
            pool.affine_select(out=ident[:, :], in_=ident[:, :], compare_op=ALU.not_equal, fill=1.0,
                               base=0, pattern=[[-1, P]], channel_multiplier=1).then_inc(ident_ready, 1)
            pool.memset(mem_w[:, :], 0.0).then_inc(mem_zero, 1)
            pool.memset(zeros[:, :], 0.0)
            pool.memset(v_head[:, :, :, :], 0.0)
            link(pool.memset(ones[:, :], 1.0))
            pool.memset(v_head[:, :, :, DH:DH + 1], 1.0)
            pool.iota(iota_e[:, :], pattern=[[1, E]], base=0, channel_multiplier=0,
                      allow_small_or_imprecise_dtypes=True)
            pool.iota(iota_t[:, :], pattern=[[1, TILES]], base=0, channel_multiplier=0,
                      allow_small_or_imprecise_dtypes=True)
            pool.iota(full_at[:, :], pattern=[[P, NT]], base=0, channel_multiplier=0,
                      allow_small_or_imprecise_dtypes=True)
            pool.affine_select(out=before[:, :], in_=ones[:, 0:P], compare_op=ALU.is_gt, fill=0.0,
                               base=0, pattern=[[1, P]], channel_multiplier=-1).then_inc(consts_ready, 1)

            pool.wait_ge(routed, 1)
            pool.wait_ge(slots_cleared, 16)
            for k in range(TOPK):
                for c in range(NT):
                    n = k * NT + c
                    pool.indirect_dma_start(
                        out=slot_x, out_offset=bass.IndirectOffsetOnAxis(ap=slot[:, n:n + 1], axis=0),
                        in_=xn[:, c, :], in_offset=None).then_inc(scattered, 16)

            pool.wait_ge(v_copied, 1)

            def stage_v(i, b, h, s):
                wait(pool, pv_done, ST * (i - 1))
                pool.tensor_copy(v_head[:, s % 2, :, 0:DH],
                                 v_all[:, bass.ds(b * ST, ST), bass.ds(h * DH, DH)]).then_inc(v_head_ready, 1)

            def split_m(i, s, pairs):
                a = s % 2
                pool.wait_ge(negm_ready, i + 1)
                wait(pool, m_loaded[a], pairs * 48)
                pool.tensor_tensor(m_parts[:, a, 0, :], negm[:, a, :], zeros[0:16, 0:P], ALU.subtract).then_inc(m_hi, 1)
                pool.wait_ge(m_hi, i + 1)
                pool.tensor_tensor(negr[:, a, :], negm[:, a, :], m_parts[:, a, 0, :], ALU.subtract).then_inc(m_res, 1)
                pool.wait_ge(m_res, i + 1)
                pool.tensor_tensor(m_parts[:, a, 1, :], negr[:, a, :], zeros[0:16, 0:P], ALU.subtract).then_inc(m_mid, 1)
                pool.wait_ge(m_mid, i + 1)
                pool.tensor_tensor(m_parts[:, a, 2, :], negr[:, a, :], m_parts[:, a, 1, :], ALU.subtract)\
                    .then_inc(m_ready, 1)

            def add_o(i, b, h, s):
                pool.wait_ge(o_ready, i + 1)
                place = acc[:, bass.ds(b * ST, ST), :].rearrange("p t (g c) -> p t g c", g=G)[
                    :, :, :, bass.ds(h * DH, DH)]
                pool.tensor_tensor(place, place, otmp[:, s % 2, :, :].rearrange("p (t g) d -> p t g d", t=ST),
                                   ALU.add).then_inc(o_added, 1)

            pool.wait_ge(mem_used, NT)

            def steps(blk, b, h0, first=False):
                for s in range(4):
                    i = blk * 4 + s
                    stage_v(i, b, h0 + s, s)
                    split_m(i, s, blk * 2 + s // 2)
                    if first and s < 2:
                        continue
                    if s >= 2:
                        add_o(i - 2, b, h0 + s - 2, s)
                    elif h0 == 4:
                        add_o(i - 2, b, h0 + s - 2, s)
                    else:
                        add_o(i - 2, b - 1, H + s - 2, s)

            steps(0, 0, 0, first=True)
            steps(1, 0, 4)
            with pool.Fori(1, BATCH) as b:
                steps(b * 2, b, 0)
                steps(b * 2 + 1, b, 4)
            add_o(STEPS - 2, BATCH - 1, H - 2, 0)
            add_o(STEPS - 1, BATCH - 1, H - 1, 1)

            for a in range(2):
                pool.wait_ge(y_stored[a], 16 * ((TILES + 1 - a) // 2))
            pool.wait_ge(y_in_psum, TILES)
            for n in range(4):
                if n > 0:
                    pool.wait_ge(s_mix, 8 * n)
                for c in range(4):
                    for k in range(TOPK):
                        w = k * NT + 4 * n + c
                        pool.indirect_dma_start(
                            out=gath[:, 2 * c + k, :], out_offset=None, in_=slot_y,
                            in_offset=bass.IndirectOffsetOnAxis(ap=slot[:, w:w + 1], axis=0)).then_inc(gathered, 16)

        @block.scalar
        def _(act):
            act.wait_ge(var_ready, 1)
            act.activation(sd[:, :], meanvar[:, :, 1], ACT.Sqrt).then_inc(sd_ready, 1)
            for n in range(0, 8, 2):
                act.wait_ge(xT_in_psum, n + 1)
                act.activation(xnT[:, n % 2, 512 * (n // 2):512 * (n // 2 + 1)], ps[:, n, :], ACT.Copy)\
                   .then_inc(xT_even, 1)
            act.wait_ge(v_in_psum, 1)
            act.activation(v_all[:, :, :].rearrange("p (a c) n -> p a (c n)", a=2), ps[:, 1:3, :], ACT.Copy)\
               .then_inc(v_copied, 1)
            act.wait_ge(small_loaded, 16)
            act.activation(mixw[:, 1:2], mixw[:, 0:1], ACT.Exp, scale=-1.0).then_inc(mix_exp, 1)
            act.wait_ge(qk_copied, 4)
            act.activation(kc[0], kf, ACT.Copy).then_inc(part_hi, 1)
            act.wait_ge(residual, 1)
            act.activation(kc[1], kr, ACT.Copy).then_inc(part_mid, 1)
            act.wait_ge(qk_copied, 12)
            act.activation(qc[0], qf, ACT.Copy).then_inc(part_hi, 1)
            act.wait_ge(residual, 2)
            act.activation(qc[1], qr, ACT.Copy).then_inc(part_mid, 1)
            act.wait_ge(q_min, 1)
            act.activation(qr, qr, ACT.Exp).then_inc(q_elu_parts, 1)
            act.activation(qf, qf, ACT.Relu).then_inc(q_elu_parts, 1)
            act.wait_ge(gap_ready, 1)
            act.activation(score[:, 1, :], score[:, 1, :], ACT.Exp).then_inc(gap_exp, 1)

            def negate_max(i, s):
                act.wait_ge(maxT_in_psum, i + 1)
                wait(act, m_ready, i - 1)
                act.activation(negm[:, s % 2, :], ps[0:16, 7, 0:P], ACT.Copy, scale=-1.0).then_inc(negm_ready, 1)

            def evacuate_o(i, s):
                act.wait_ge(pv_done, ST * (i + 1))
                wait(act, oT_in_psum, i - 1)
                act.activation(o_sb[:, s % 2, :], ps[:, 6, :], ACT.Copy).then_inc(o_copied, 1)

            def exps(i, s, last=False):
                for u in range(16):
                    t, g = divmod(u, G)
                    if u == 2 and not (isinstance(i, int) and i == 0):
                        evacuate_o(i - 1, s + 1)
                    if u == 4 and not last:
                        negate_max(i + 1, s + 1)
                    act.wait_ge(scores_ready, i * 16 + (u + 1))
                    if g == 0:
                        wait(act, pv_done, i * ST + (t - 1))
                    act.activation(probs[:, t % 2, g, :], ps[:, 4 + u % 2, :], ACT.Exp, scale=SCALE)\
                       .then_inc(probs_ready, 1)

            act.wait_ge(mem_in_psum, NT)
            act.wait_ge(stacks_written, 16 * NC * (1 + KD))
            for n in range(2):
                act.dma_start(w1_sb[:, 4 * n:4 * n + 4, :, :].rearrange("p e k n -> p (e k) n"),
                              w1[4 * n:4 * n + 4].rearrange("e (k p) n -> p (e k) n", p=P)).then_inc(w12_loaded, 16)
                act.dma_start(w2_sb[:, 4 * n:4 * n + 4, :, :].rearrange("p e k n -> p (e k) n"),
                              w2[4 * n:4 * n + 4].rearrange("e (k p) n -> p (e k) n", p=P)).then_inc(w12_loaded, 16)

            negate_max(0, 0)
            for i in range(4):
                exps(i, i)
            with act.Fori(1, NLOOP - 1) as blk:
                for s in range(4):
                    exps(blk * 4 + s, s)
            for i in range(STEPS - 4, STEPS):
                exps(i, i % 4, last=i == STEPS - 1)
            evacuate_o(STEPS - 1, 1)

            act.wait_ge(scattered, 16 * TOPK * NT)

            def copy_xT(j, a):
                act.wait_ge(exT_in_psum, j + 1)
                wait(act, up_done, (j - 1) * 2)
                act.activation(e_xT[:, a, :, :], ps[:, 4, 0:D].rearrange("p (k n) -> p k n", k=KD), ACT.Copy)\
                   .then_inc(exT_ready, 1)

            def silu_g(j, a):
                act.wait_ge(up_done, j * 2 + 1)
                wait(act, h_ready, j - 1)
                act.activation(e_silu[:, a, :], ps[:, 2 * a, :], ACT.Silu).then_inc(silu_done, 1)

            def copy_y(j, pair, a):
                act.wait_ge(y_in_psum, j + 1)
                wait(act, y_stored[a], pair * 16)
                act.activation(e_y[:, a, :], ps[:, 6 + a, 0:D], ACT.Copy).then_inc(y_ready, 1)

            def tile(j, pair, a):
                if live(j):
                    silu_g(j, a)
                if live(j + 1):
                    copy_xT(j + 1, 1 - a)
                if live(j - 2):
                    copy_y(j - 2, pair - 1, a)

            copy_xT(0, 0)
            over_tiles(act, tile)

            with act.Fori(0, NT // 4) as n:
                for f in range(NF):
                    act.wait_ge(s_up, n * (2 * NF) + (2 * f + 1))
                    act.wait_ge(s_h, n * NF + max(f - 1, 0))
                    act.activation(sh_silu[:, f % 2, :], ps[:, f % 2, :], ACT.Silu).then_inc(s_silu, 1)

        @block.vector
        def _(dve):
            count = [0]

            def link(ins):
                count[0] += 1
                ins.then_inc(dve_step, 1)
                dve.wait_ge(dve_step, count[0])

            for c in range(NT):
                if c % 4 == 0:
                    dve.wait_ge(x_loaded[c // 4], 16)
                last = dve.bn_stats(stats[:, c, :], acc[:, c, :])
            link(last)
            for c in range(NT):
                last = dve.bn_aggr(meanvar[:, c, :], stats[:, c, :])
            link(last)
            dve.tensor_scalar_add(meanvar[:, :, 1], meanvar[:, :, 1], EPS).then_inc(var_ready, 1)
            dve.wait_ge(sd_ready, 1)
            link(dve.reciprocal(rstd[:, :], sd[:, :]))
            for c in range(NT):
                dve.tensor_scalar(xn[:, c, :], acc[:, c, :], meanvar[:, c, 0:1], rstd[:, c:c + 1],
                                  ALU.subtract, ALU.mult).then_inc(xn_ready, 1)
            for n in range(1, 8, 2):
                dve.wait_ge(xT_in_psum, n + 1)
                dve.tensor_copy(xnT[:, n % 2, 512 * (n // 2):512 * (n // 2 + 1)], ps[:, n, :]).then_inc(xT_odd, 1)

            for u in range(12):
                dve.wait_ge(qk_in_psum, u + 1)
                bank = 3 + u % 4
                if u < 4:
                    ins = dve.tensor_copy(kf[:, 512 * u:512 * (u + 1)], ps[0:DKV, bank, :])
                else:
                    m, n = divmod(u - 4, 4)
                    ins = dve.tensor_copy(qf[:, m, 512 * n:512 * (n + 1)], ps[:, bank, :])
                ins.then_inc(qk_copied, 1)

            dve.wait_ge(logits_in_psum, 1)
            link(dve.tensor_copy(logits[:, :, :], ps[:, 0, 0:NT * E].rearrange("p (c e) -> p c e", c=NT)))
            for c in range(NT):
                last = dve.max(top[:, c, :], logits[:, c, :])
            link(last)
            for c in range(NT):
                last = dve.max_index(topi[:, c, :], top[:, c, :], logits[:, c, :])
            link(last)
            dve.tensor_tensor(score[:, 1, :], top[:, :, 1], top[:, :, 0], ALU.subtract).then_inc(gap_ready, 1)
            link(dve.tensor_copy(choice[:, :, :], topi[:, :, 0:TOPK].rearrange("p c k -> p k c")))
            dve.wait_ge(consts_ready, 1)
            W = TOPK * NT
            dve.tensor_tensor(onehot[:, :, :],
                              choice[:, :, :].rearrange("p k c -> p (k c)").unsqueeze(2).to_broadcast([P, W, E]),
                              iota_e[:, :].unsqueeze(1).to_broadcast([P, W, E]), ALU.is_equal)\
               .then_inc(onehot_ready, 1)

            def parts(f, r, c, n):
                dve.wait_ge(part_hi, n)
                dve.tensor_tensor(r, f, c[0], ALU.subtract).then_inc(residual, 1)
                dve.wait_ge(part_mid, n)
                dve.wait_ge(residual, n)
                dve.tensor_tensor(c[2], r, c[1], ALU.subtract).then_inc(part_lo, 1)

            parts(kf, kr, kc, 1)
            parts(qf, qr, qc, 2)
            dve.wait_ge(part_lo, 2)
            dve.tensor_scalar_min(qr, qf, 0.0).then_inc(q_min, 1)

            dve.wait_ge(ranks_in_psum, 1)
            dve.tensor_copy(rank[:, :, :].rearrange("p w e -> p (w e)"), ps[:, 7, 0:W * E])
            link(dve.tensor_copy(total[:, :, :].rearrange("p w e -> p (w e)"), ps[:, 7, W * E:2 * W * E]))
            src, dst, other = total, run_a, run_b
            step = 1
            while step < W:
                dve.tensor_copy(dst[:, 0:step, :], src[:, 0:step, :])
                link(dve.tensor_tensor(dst[:, step:W, :], src[:, step:W, :], src[:, 0:W - step, :], ALU.add))
                src, dst, other = dst, other, dst
                step *= 2
            link(dve.tensor_tensor(gt[:, :, :], src[:, W - 1, :].unsqueeze(2).to_broadcast([P, E, NT]),
                                   full_at[:, :].unsqueeze(1).to_broadcast([P, E, NT]), ALU.is_gt))
            link(dve.tensor_reduce(tiles_e[:, :], gt[:, :, :], X_AXIS, ALU.add))
            csrc, cdst, cother = tiles_e, cum_a, cum_b
            step = 1
            while step < E:
                dve.tensor_copy(cdst[:, 0:step], csrc[:, 0:step])
                link(dve.tensor_tensor(cdst[:, step:E], csrc[:, step:E], csrc[:, 0:E - step], ALU.add))
                csrc, cdst, cother = cdst, cother, cdst
                step *= 2
            link(dve.tensor_tensor(le[:, :, :], csrc[:, :].unsqueeze(1).to_broadcast([P, TILES, E]),
                                   iota_t[:, :].unsqueeze(2).to_broadcast([P, TILES, E]), ALU.is_le))
            link(dve.tensor_reduce(expert_f[:, :], le[:, :, :], X_AXIS, ALU.add))
            dve.tensor_scalar_min(expert[:, :], expert_f[:, :], float(E - 1))
            link(dve.tensor_tensor(cdst[:, :], csrc[:, :], tiles_e[:, :], ALU.subtract))
            link(dve.tensor_tensor(dst[:, :, :], src[:, :, :], total[:, :, :], ALU.subtract))
            link(dve.tensor_tensor(rank[:, :, :], rank[:, :, :], dst[:, :, :], ALU.add))
            link(dve.scalar_tensor_tensor(dst[:, :, :], cdst[:, :].unsqueeze(1).to_broadcast([P, W, E]), float(P),
                                          rank[:, :, :], ALU.mult, ALU.add))
            link(dve.tensor_tensor(rank[:, :, :], dst[:, :, :], onehot[:, :, :], ALU.mult))
            link(dve.tensor_reduce(slot_f[:, :], rank[:, :, :], X_AXIS, ALU.add))
            dve.tensor_copy(slot[:, :], slot_f[:, :]).then_inc(routed, 1)
            dve.wait_ge(gap_exp, 1)
            link(dve.tensor_scalar_add(score[:, 0, :], score[:, 1, :], 1.0))
            link(dve.reciprocal(score[:, 0, :], score[:, 0, :]))
            dve.tensor_tensor(score[:, 1, :], score[:, 1, :], score[:, 0, :], ALU.mult)
            dve.wait_ge(mix_exp, 1)
            link(dve.tensor_scalar_add(mixw[:, 2:3], mixw[:, 1:2], 1.0))
            link(dve.reciprocal(mixw[:, 2:3], mixw[:, 2:3]))
            link(dve.tensor_scalar(mixw[:, 3:4], mixw[:, 2:3], -1.0, 1.0, ALU.mult, ALU.add))
            dve.wait_ge(q_elu_parts, 2)
            dve.scalar_tensor_tensor(qf, qr, 1.0, qf, ALU.subtract, ALU.add).then_inc(sigma_ready, 1)
            for c in range(NT):
                dve.wait_ge(mem_in_psum, c + 1)
                read = ps[:, 3 + c % 4, 0:G * MEMW].rearrange("p (g n) -> p g n", g=G)
                link(dve.reciprocal(mden[:, c % 2, :], read[:, :, DKV]))
                link(dve.scalar_tensor_tensor(
                    mtmp[:, c % 2, :].rearrange("p (g n) -> p g n", g=G), read[:, :, 0:DKV], mixw[:, 2:3],
                    mden[:, c % 2, :].unsqueeze(2).to_broadcast([P, G, DKV]), ALU.mult, ALU.mult))
                dve.tensor_tensor(acc[:, c, :], acc[:, c, :], mtmp[:, c % 2, :], ALU.add).then_inc(mem_used, 1)

            def maxima(i, s, pair):
                dve.wait_ge(a_ready, i * 8 + (pair + 1))
                if pair == 0:
                    wait(dve, maxT_in_psum, i - 1)
                b = 2 * (pair % 2)
                dve.reduce_max(smax[:, s % 2, 2 * pair:2 * pair + 2], ps[:, b:b + 2, :], X_AXIS).then_inc(max_done, 1)

            def finish_o(i, s):
                a = s % 2
                dve.wait_ge(oT_in_psum, i + 1)
                wait(dve, o_added, i - 1)
                o = ps[:, 7, :].rearrange("p (w n) -> p w n", n=32)
                dve.reciprocal(rden[:, a, :], o[:, :, DH]).then_inc(rden_ready, 1)
                dve.wait_ge(rden_ready, i + 1)
                dve.scalar_tensor_tensor(otmp[:, a, :, :], o[:, :, 0:DH], mixw[:, 3:4],
                                         rden[:, a, :].unsqueeze(2).to_broadcast([P, 16, DH]), ALU.mult, ALU.mult)\
                   .then_inc(o_ready, 1)

            def step(i, s, first=False, ahead=True):
                for pair in range(8):
                    if pair == 4 and not first:
                        finish_o(i - 1, s + 1)
                    if ahead:
                        maxima(i + 2, s, pair)

            for i in range(2):
                for pair in range(8):
                    maxima(i, i, pair)
            for i in range(4):
                step(i, i, first=i == 0)
            with dve.Fori(1, NLOOP - 1) as blk:
                for s in range(4):
                    step(blk * 4 + s, s)
            for i in range(STEPS - 4, STEPS):
                step(i, i % 4, ahead=i + 2 < STEPS)
            finish_o(STEPS - 1, STEPS - 1)

            def copy_hT(j, a):
                dve.wait_ge(hT_in_psum, j + 1)
                wait(dve, y_in_psum, j - 1)
                dve.tensor_copy(e_hT[:, a, :, :].rearrange("p k n -> p (k n)"), ps[:, 5, :]).then_inc(hT_ready, 1)

            def make_h(j, a):
                dve.wait_ge(silu_done, j + 1)
                dve.wait_ge(up_done, j * 2 + 2)
                wait(dve, hT_in_psum, j - 1)
                dve.tensor_tensor(e_h[:, a, :], e_silu[:, a, :], ps[:, 2 * a + 1, :], ALU.mult).then_inc(h_ready, 1)

            def tile(j, pair, a):
                if live(j - 1):
                    copy_hT(j - 1, 1 - a)
                if live(j):
                    make_h(j, a)

            over_tiles(dve, tile)

            dve.wait_ge(y_in_psum, TILES)
            dve.wait_ge(o_added, STEPS)
            with dve.Fori(0, NT // 4) as n:
                for f in range(NF):
                    dve.wait_ge(s_silu, n * NF + (f + 1))
                    dve.wait_ge(s_up, n * (2 * NF) + (2 * f + 2))
                    dve.wait_ge(s_hused, n * NF + max(f - 1, 0))
                    dve.tensor_tensor(sh_h[:, f % 2, :], sh_silu[:, f % 2, :], ps[:, 2 + f % 2, :], ALU.mult)\
                       .then_inc(s_h, 1)
                dve.wait_ge(s_hused, n * NF + NF)
                for c in range(4):
                    row = acc[:, bass.ds(n * 4 + c, 1), :].rearrange("p o d -> p (o d)")
                    dve.tensor_tensor(row, row, ps[:, 4 + c, 0:D], ALU.add).then_inc(s_add, 1)
                dve.wait_ge(gathered, n * (16 * 8) + 16 * 8)
                for k in range(TOPK):
                    for c in range(4):
                        row = acc[:, bass.ds(n * 4 + c, 1), :].rearrange("p o d -> p (o d)")
                        if k == 0:
                            dve.wait_ge(s_add, n * 4 + (c + 1))
                        else:
                            dve.wait_ge(s_mix, n * 8 + (c + 1))
                        dve.scalar_tensor_tensor(row, gath[:, 2 * c + k, :], score[:, k, bass.ds(n * 4 + c, 1)], row,
                                                 ALU.mult, ALU.add).then_inc(s_mix, 1)

        @block.tensor
        def _(pe):
            pe.wait_ge(ident_ready, 1)
            for n in range(8):
                m, g = n % 2, n // 2
                pe.wait_ge(xn_ready, 4 * g + 4)
                for c in range(4):
                    last = pe.transpose(ps[:, n, P * c:P * (c + 1)], xn[:, 4 * g + c, P * m:P * (m + 1)], ident[:, :])
                last.then_inc(xT_in_psum, 1)
            pe.wait_ge(proj_loaded, 64)
            pe.wait_ge(xT_even, 4)
            pe.wait_ge(xT_odd, 4)
            for c in range(NT):
                for k in range(KD):
                    last = pe.matmul(ps[:, 0, E * c:E * (c + 1)], xnT[:, k, P * c:P * (c + 1)], router[:, k, :],
                                     start=k == 0, stop=k == KD - 1)
            last.then_inc(logits_in_psum, 1)
            for c in range(NT):
                for k in range(KD):
                    last = pe.matmul(ps[:, 1 + c // 8, DKV * (c % 8):DKV * (c % 8 + 1)], xnT[:, k, P * c:P * (c + 1)],
                                     wv_sb[:, k, :], start=k == 0, stop=k == KD - 1)
            last.then_inc(v_in_psum, 1)
            for u in range(12):
                wait(pe, qk_copied, u - 3)
                for k in range(KD):
                    if u < 4:
                        last = pe.matmul(ps[0:DKV, 3 + u % 4, :], wk_sb[:, k, :], xnT[:, k, 512 * u:512 * (u + 1)],
                                         start=k == 0, stop=k == KD - 1)
                    else:
                        m, n = divmod(u - 4, 4)
                        last = pe.matmul(ps[:, 3 + u % 4, :], wq_sb[:, k, P * m:P * (m + 1)],
                                         xnT[:, k, 512 * n:512 * (n + 1)], start=k == 0, stop=k == KD - 1)
                last.then_inc(qk_in_psum, 1)
            pe.wait_ge(onehot_ready, 1)
            W = TOPK * NT
            flags = onehot[:, :, :].rearrange("p w e -> p (w e)")
            pe.matmul(ps[:, 7, 0:W * E], before[:, :], flags, start=True, stop=True)
            pe.matmul(ps[:, 7, W * E:2 * W * E], ones[:, 0:P], flags, start=True, stop=True)\
              .then_inc(ranks_in_psum, 1)
            pe.wait_ge(mem_loaded, 64)
            pe.wait_ge(sigma_ready, 1)
            for c in range(NT):
                wait(pe, mem_used, c - 3)
                for m in range(KD):
                    last = pe.matmul(ps[:, 3 + c % 4, 2 * MEMW * m:2 * MEMW * (m + 1)], qf[:, m, P * c:P * (c + 1)],
                                     mem_w[:, :], start=True, stop=True)
                last.then_inc(mem_in_psum, 1)

            pe.wait_ge(mem_used, NT)
            pe.wait_ge(v_copied, 1)
            pe.wait_ge(routed, 1)
            pe.wait_ge(ones_rows, 64)

            def scores_for_max(i, s, blk, u):
                pair = u // 2
                if u == 0:
                    pe.wait_ge(stack_loaded[s], blk * 32 + 32)
                if u % 2 == 0:
                    wait(pe, max_done, i * 8 + (pair - 1))
                g, st = divmod(u, ST)
                ins = pe.matmul(ps[:, 2 * (pair % 2) + u % 2, :], q_st[s][0:R, g, P * st:P * (st + 1)],
                                k_st[s][0:R, :], start=True, stop=True)
                if u % 2:
                    ins.then_inc(a_ready, 1)

            def transpose_max(i, s):
                pe.wait_ge(max_done, i * 8 + 8)
                wait(pe, o_ready, i - 2)
                wait(pe, negm_ready, i)
                pe.transpose(ps[0:16, 7, 0:P], smax[:, s % 2, :], ident[:, :]).then_inc(maxT_in_psum, 1)

            def transpose_o(i, s):
                pe.wait_ge(o_copied, i + 1)
                wait(pe, o_ready, i)
                if ahead_of(i):
                    pe.wait_ge(negm_ready, i + 3)
                for st in range(ST):
                    last = pe.transpose(ps[:, 7, P * st:P * (st + 1)], o_sb[:, s % 2, P * st:P * (st + 1)], ident[:, :])
                last.then_inc(oT_in_psum, 1)

            def ahead_of(i):
                return not isinstance(i, int) or i + 2 < STEPS

            def weighted_values(i, s, t):
                pe.wait_ge(probs_ready, i * 16 + 4 * (t + 1))
                if t == 0:
                    pe.wait_ge(v_head_ready, i + 1)
                    wait(pe, o_copied, i)
                for g in range(G):
                    last = pe.matmul(ps[32 * g:32 * (g + 1), 6, :], v_head[:, s % 2, t, :], probs[:, t % 2, g, :],
                                     start=t == 0, stop=t == ST - 1)
                last.then_inc(pv_done, 1)

            def step(i, s, blk, first=False, ahead=True, last=False):
                pe.wait_ge(m_loaded[s % 2], blk * 96 + 48 * (s // 2 + 1))
                for t in range(ST):
                    for g in range(G):
                        u = G * t + g
                        wait(pe, probs_ready, i * 16 + (u - 1))
                        ins = pe.matmul(ps[:, 4 + u % 2, :], k_st[s][0:RM, P * t:P * (t + 1)], q_st[s][0:RM, g, :],
                                        start=True, stop=True)
                        ins.then_inc(scores_ready, 1)
                        if u == 0 and not last:
                            transpose_max(i + 1, s + 1)
                        if ahead:
                            scores_for_max(i + 2, (s + 2) % 4, blk + (s + 2) // 4, u)
                    if t == 1 and not first:
                        transpose_o(i - 1, s + 1)
                    if t >= 1:
                        weighted_values(i, s, t - 1)
                weighted_values(i, s, ST - 1)

            for i in range(2):
                for u in range(16):
                    scores_for_max(i, i, 0, u)
            transpose_max(0, 0)
            for i in range(4):
                step(i, i, 0, first=i == 0)
            with pe.Fori(1, NLOOP - 1) as blk:
                for s in range(4):
                    step(blk * 4 + s, s, blk)
            for i in range(STEPS - 4, STEPS):
                step(i, i % 4, NLOOP - 1, ahead=i + 2 < STEPS, last=i == STEPS - 1)
            transpose_o(STEPS - 1, STEPS - 1)

            pe.wait_ge(o_ready, STEPS)
            pe.wait_ge(w12_loaded, 16 * 4)

            def transpose_x(j, pair, a):
                pe.wait_ge(ex_loaded[a], pair * 16 + 16)
                wait(pe, exT_ready, j)
                for k in range(KD):
                    last = pe.transpose(ps[:, 4, P * k:P * (k + 1)], e_x[:, a, P * k:P * (k + 1)], ident[:, :])
                last.then_inc(exT_in_psum, 1)

            def up(j, a):
                e = pe.value_load(expert[0:1, bass.ds(j, 1)], min_val=0, max_val=E - 1)
                pe.wait_ge(exT_ready, j + 1)
                wait(pe, h_ready, j - 1)
                for n in range(2):
                    for k in range(KD):
                        w = w1_sb[:, bass.ds(e, 1), k, F * n:F * (n + 1)].rearrange("p o n -> p (o n)")
                        last = pe.matmul(ps[:, 2 * a + n, :], e_xT[:, a, k, :], w, start=k == 0, stop=k == KD - 1)
                    last.then_inc(up_done, 1)

            def transpose_h(j, a):
                pe.wait_ge(h_ready, j + 1)
                wait(pe, hT_ready, j)
                for k in range(F // P):
                    last = pe.transpose(ps[:, 5, P * k:P * (k + 1)], e_h[:, a, P * k:P * (k + 1)], ident[:, :])
                last.then_inc(hT_in_psum, 1)

            def down(j, a):
                e = pe.value_load(expert[0:1, bass.ds(j, 1)], min_val=0, max_val=E - 1)
                pe.wait_ge(hT_ready, j + 1)
                wait(pe, y_ready, j - 1)
                for k in range(F // P):
                    w = w2_sb[:, bass.ds(e, 1), k, :].rearrange("p o n -> p (o n)")
                    last = pe.matmul(ps[:, 6 + a, 0:D], e_hT[:, a, k, :], w, start=k == 0, stop=k == F // P - 1)
                last.then_inc(y_in_psum, 1)

            def tile(j, pair, a):
                if live(j):
                    up(j, a)
                if live(j - 1):
                    transpose_h(j - 1, 1 - a)
                if live(j + 1):
                    transpose_x(j + 1, pair + a, 1 - a)
                if live(j - 2):
                    down(j - 2, a)

            transpose_x(0, 0, 0)
            over_tiles(pe, tile)

            pe.wait_ge(shw_loaded, 48)
            pe.wait_ge(y_ready, TILES)
            with pe.Fori(0, NT // 4) as n:
                def shared_down(f):
                    pe.wait_ge(s_h, n * NF + (f + 1))
                    if f == 0:
                        pe.wait_ge(s_add, n * 4)
                    for c in range(4):
                        last = pe.matmul(ps[:, 4 + c, 0:D], sh_h[:, f % 2, P * c:P * (c + 1)], wd_sb[:, f, :],
                                         start=f == 0, stop=f == NF - 1)
                    last.then_inc(s_hused, 1)

                for f in range(NF):
                    pe.wait_ge(s_h, n * NF + max(f - 1, 0))
                    for w, bank in ((wg_sb, f % 2), (wu_sb, 2 + f % 2)):
                        for k in range(KD):
                            last = pe.matmul(ps[:, bank, :], w[:, k, P * f:P * (f + 1)],
                                             xnT[:, k, bass.ds(n * 512, 512)], start=k == 0, stop=k == KD - 1)
                        last.then_inc(s_up, 1)
                    if f > 0:
                        shared_down(f - 1)
                shared_down(NF - 1)


def kernel(L0_attn_x, L0_attn_Wq, L0_attn_Wk, L0_attn_Wv, L0_attn_memory, L0_attn_memory_norm, L0_attn_memory_weight,
           L0_ffn_router_w, L0_ffn_w1, L0_ffn_w2, L0_ffn_w_gate, L0_ffn_w_up, L0_ffn_w_down):
    import concourse.bacc as bacc
    from concourse.bass_utils import run_bass_kernel_spmd

    arrays = {
        "x": L0_attn_x, "wqT": np.asarray(L0_attn_Wq).T, "wkT": np.asarray(L0_attn_Wk).T,
        "wvT": np.asarray(L0_attn_Wv).T, "memory": L0_attn_memory, "memory_norm": L0_attn_memory_norm,
        "memory_weight": L0_attn_memory_weight, "router_w": L0_ffn_router_w, "w1": L0_ffn_w1, "w2": L0_ffn_w2,
        "w_gate": L0_ffn_w_gate, "w_up": L0_ffn_w_up, "w_down": L0_ffn_w_down,
    }
    arrays = {name: np.ascontiguousarray(a) for name, a in arrays.items()}
    nc = bacc.Bacc("TRN2", target_bir_lowering=False, num_devices=1)
    args = [nc.dram_tensor(name, a.shape, mybir.dt.from_np(a.dtype), kind="ExternalInput").ap()
            for name, a in arrays.items()]
    out = nc.dram_tensor("out", arrays["x"].shape, F32, kind="ExternalOutput").ap()
    build(nc, *args, out)
    result = run_bass_kernel_spmd(nc, [arrays], core_ids=[0])
    return result.results[0]["out"]
```

```python
from contextlib import ExitStack

import numpy as np

import concourse.bass as bass
from concourse import mybir

F32 = mybir.dt.float32
BF16 = mybir.dt.bfloat16
I32 = mybir.dt.int32
U32 = mybir.dt.uint32
ALU = mybir.AluOpType
ACT = mybir.ActivationFunctionType
X_AXIS = mybir.AxisListType.X

P = 128


def wait(eng, sem, value):
    if isinstance(value, int) and value <= 0:
        return
    eng.wait_ge(sem, value)


def build(nc, x, wqT, wkT, wvT, memory, memory_norm, memory_weight, router_w, w1, w2, w_gate, w_up, w_down, out):
    BATCH, SEQ, D = x.shape
    T = BATCH * SEQ
    NT = T // P
    KD = D // P
    DKV = wkT.shape[1]
    DH = 8
    H = DKV // DH
    G = D // DKV
    ST = SEQ // P
    STEPS = BATCH * H
    E, _, F2 = w1.shape
    F = F2 // 2
    FS = w_gate.shape[1]
    TOPK = 2
    TILES = (T * TOPK + E * (P - 1)) // P
    SLOTS = TILES * P
    SCALE = float(np.float32(1.0 / np.sqrt(np.float32(DH))))
    EPS = 1e-5
    Q_PART = (0, 0, 0, 1, 1, 1, 2, 2, 2)
    K_PART = (0, 1, 2, 0, 1, 2, 0, 1, 2)
    NC = len(Q_PART)
    R = NC * DH
    RM = R + 3
    MEMW = DKV + 1
    VW = DKV + E
    VT = 512 // VW
    assert (D, DKV, H, G, ST, E, F, FS, TILES) == (256, 64, 8, 4, 4, 8, 512, 1024, 39)

    q_stacks = nc.dram_tensor("q_stacks", [G, H, R, T], BF16, kind="Internal").ap()
    k_stacks = nc.dram_tensor("k_stacks", [H, R, T], BF16, kind="Internal").ap()
    slot_x = nc.dram_tensor("slot_x", [SLOTS, D], F32, kind="Internal").ap()
    slot_y = nc.dram_tensor("slot_y", [SLOTS, D], F32, kind="Internal").ap()

    x_rows = x.rearrange("b s d -> (b s) d")
    out_rows = out.rearrange("b s d -> (b s) d")

    with ExitStack() as ctx:
        def sb(name, shape, dt=F32):
            return ctx.enter_context(nc.sbuf_tensor(name, shape, dt))

        def sem(name):
            return ctx.enter_context(nc.semaphore(name))

        ps = ctx.enter_context(nc.psum_tensor("ps", [P, 8, 512], F32))

        acc = sb("acc", [P, NT, D])
        xn = sb("xn", [P, NT, D])
        xnT = sb("xnT", [P, KD, T])
        big = sb("big", [P, 24576])
        att = sb("att", [P, 9216])
        o_sb = sb("o_sb", [P, 2, 512])
        vl_all = sb("vl_all", [P, NT, DKV + E])
        v_all = vl_all[:, :, 0:DKV]
        logits = vl_all[:, :, DKV:DKV + E]
        v_head = sb("v_head", [P, 2, ST, 32])
        ident = sb("ident", [P, P])
        before = sb("before", [P, P], BF16)
        ones = sb("ones", [P, 512], BF16)
        zeros = sb("zeros", [P, D])
        mem_w = sb("mem_w", [P, 2 * MEMW])
        mixw = sb("mixw", [P, 4])
        stats = sb("stats", [P, NT, 6])
        meanvar = sb("meanvar", [P, NT, 2])
        sd = sb("sd", [P, NT])
        rstd = sb("rstd", [P, NT])
        top = sb("top", [P, NT, 8])
        topi = sb("topi", [P, NT, 8], U32)
        choice = sb("choice", [P, TOPK, NT])
        score = sb("score", [P, TOPK, NT])
        iota_e = sb("iota_e", [P, E])
        iota_t = sb("iota_t", [P, TILES])
        full_at = sb("full_at", [P, NT])
        onehot = sb("onehot", [P, TOPK * NT, E], BF16)
        tiles_e = sb("tiles_e", [P, E])
        cum_a = sb("cum_a", [P, E])
        cum_b = sb("cum_b", [P, E])
        slot_f = sb("slot_f", [P, TOPK * NT])
        slot = sb("slot", [P, TOPK * NT], U32)
        expert_f = sb("expert_f", [P, TILES])
        expert = sb("expert", [P, TILES], I32)
        mden = sb("mden", [P, 2, G])
        smax = sb("smax", [P, 2, 16])
        negm = sb("negm", [16, 2, P])
        negr = sb("negr", [16, 2, P])
        m_parts = sb("m_parts", [16, 2, 3, P], BF16)
        rden = sb("rden", [P, 2, 16])
        oT_sb = sb("oT_sb", [P, 2, 16, DH + 1])
        otmp = sb("otmp", [P, 2, 16, DH])
        e_x = sb("e_x", [P, 2, D])

        rank, total, run_a, run_b = [big[:, 22288 + 256 * n:22544 + 256 * n].rearrange("p (w e) -> p w e", e=E)
                                     for n in range(4)]
        gt = big[:, 23312:23440].rearrange("p (e c) -> p e c", e=E)
        le = big[:, 23440:23440 + TILES * E].rearrange("p (j e) -> p j e", e=E)
        mtmp = big[:, 23808:23808 + 2 * D].rearrange("p (a d) -> p a d", a=2)
        qf = big[:, 0:4096].rearrange("p (m t) -> p m t", m=KD)
        qr = big[:, 4096:8192].rearrange("p (m t) -> p m t", m=KD)
        qc = [big[:, 8192 + 2048 * n:8192 + 2048 * (n + 1)].bitcast(BF16).rearrange("p (m t) -> p m t", m=KD)
              for n in range(3)]
        kf = big[0:DKV, 14336:16384]
        kr = big[0:DKV, 16384:18432]
        qe = big[:, 14336:18432].rearrange("p (m t) -> p m t", m=KD)
        kc = [big[0:DKV, 18432 + 1024 * n:18432 + 1024 * (n + 1)].bitcast(BF16) for n in range(3)]
        wq_sb = big[:, 21504:22016].rearrange("p (k n) -> p k n", k=KD)
        wk_sb = big[:, 22016:22144].rearrange("p (k n) -> p k n", k=KD)
        wvr_sb = big[:, 22144:22288].rearrange("p (k n) -> p k n", k=KD)
        w1_sb = big[:, 0:16384].rearrange("p (e k n) -> p e k n", e=E, k=KD)
        w2_sb = big[:, 16384:24576].rearrange("p (e k n) -> p e k n", e=E, k=F // P)
        probs = att[:, 0:4096].rearrange("p (a g s) -> p a g s", a=2, g=G)
        q_st = [att[:, 4096 + 1024 * n:5120 + 1024 * n].bitcast(BF16).rearrange("p (g s) -> p g s", g=G)
                for n in range(4)]
        k_st = [att[:, 8192 + 256 * n:8448 + 256 * n].bitcast(BF16) for n in range(4)]
        wg_sb = att[:, 0:2048].rearrange("p (k n) -> p k n", k=KD)
        wu_sb = att[:, 2048:4096].rearrange("p (k n) -> p k n", k=KD)
        wd_sb = att[:, 4096:6144].rearrange("p (k n) -> p k n", k=FS // P)
        sh_silu = att[:, 6144:7168].rearrange("p (a n) -> p a n", a=2)
        sh_h = att[:, 7168:8192].rearrange("p (a n) -> p a n", a=2)
        xnf = xn[:, :, :].rearrange("p c d -> p (c d)")
        e_xT = xnf[:, 0:512].rearrange("p (a k n) -> p a k n", a=2, k=KD)
        e_silu = xnf[:, 512:1536].rearrange("p (a n) -> p a n", a=2)
        e_h = xnf[:, 1536:2560].rearrange("p (a n) -> p a n", a=2)
        e_hT = xnf[:, 2560:3584].rearrange("p (a k n) -> p a k n", a=2, k=F // P)
        e_y = xnf[:, 3584:4096].rearrange("p (a n) -> p a n", a=2)
        gath = xnf.rearrange("p (a w n) -> p a w n", a=2, w=8)

        x_loaded = [sem(f"x_loaded{n}") for n in range(4)]
        proj_loaded = sem("proj_loaded")
        small_loaded = sem("small_loaded")
        mem_loaded = sem("mem_loaded")
        mem_zero = sem("mem_zero")
        ident_zero = sem("ident_zero")
        ident_ready = sem("ident_ready")
        consts_ready = sem("consts_ready")
        slots_cleared = sem("slots_cleared")
        dve_step = sem("dve_step")
        act_step = sem("act_step")
        pool_step = sem("pool_step")
        var_ready = sem("var_ready")
        sd_ready = sem("sd_ready")
        xn_ready = sem("xn_ready")
        xT_in_psum = sem("xT_in_psum")
        xT_copied = sem("xT_copied")
        vl_in_psum = sem("vl_in_psum")
        vl_copied = sem("vl_copied")
        qk_in_psum = sem("qk_in_psum")
        qk_copied = sem("qk_copied")
        part_hi = sem("part_hi")
        residual = sem("residual")
        part_mid = sem("part_mid")
        part_lo = sem("part_lo")
        stacks_written = sem("stacks_written")
        q_min = sem("q_min")
        q_elu_parts = sem("q_elu_parts")
        sigma_ready = sem("sigma_ready")
        mem_in_psum = sem("mem_in_psum")
        mem_used = sem("mem_used")
        mem_added = sem("mem_added")
        experts_known = sem("experts_known")
        ranks_copied = sem("ranks_copied")
        mix_exp = sem("mix_exp")
        gap_ready = sem("gap_ready")
        gap_exp = sem("gap_exp")
        onehot_ready = sem("onehot_ready")
        ranks_in_psum = sem("ranks_in_psum")
        routed = sem("routed")
        scattered = sem("scattered")

        ones_rows = sem("ones_rows")
        stack_loaded = [sem(f"stack_loaded{n}") for n in range(4)]
        m_loaded = [sem(f"m_loaded{n}") for n in range(2)]
        a_ready = sem("a_ready")
        max_done = sem("max_done")
        maxT_in_psum = sem("maxT_in_psum")
        negm_ready = sem("negm_ready")
        m_hi = sem("m_hi")
        m_res = sem("m_res")
        m_mid = sem("m_mid")
        m_ready = sem("m_ready")
        scores_ready = sem("scores_ready")
        probs_ready = sem("probs_ready")
        v_head_ready = sem("v_head_ready")
        pv_done = sem("pv_done")
        o_copied = sem("o_copied")
        oT_in_psum = sem("oT_in_psum")
        oT_copied = sem("oT_copied")
        rden_ready = sem("rden_ready")
        o_ready = sem("o_ready")
        o_added = sem("o_added")

        w12_loaded = sem("w12_loaded")
        ex_loaded = [sem(f"ex_loaded{n}") for n in range(2)]
        exT_in_psum = sem("exT_in_psum")
        exT_ready = sem("exT_ready")
        up_done = sem("up_done")
        silu_done = sem("silu_done")
        h_ready = sem("h_ready")
        hT_in_psum = sem("hT_in_psum")
        hT_ready = sem("hT_ready")
        y_in_psum = sem("y_in_psum")
        y_ready = sem("y_ready")
        y_stored = [sem(f"y_stored{n}") for n in range(2)]
        shw_loaded = sem("shw_loaded")

        gathered = [sem(f"gathered{a}") for a in range(2)]
        s_up = sem("s_up")
        s_silu = sem("s_silu")
        s_h = sem("s_h")
        s_hused = sem("s_hused")
        s_down = sem("s_down")
        s_add = sem("s_add")
        s_mix = sem("s_mix")
        stored = sem("stored")

        block = ctx.enter_context(nc.Block())
        NF = FS // P

        RING = (4, 5, 7)
        TURNS, MAX_AT, OUT_AT = 18, 4, 9

        def turn_of(u):
            return u + (u >= MAX_AT) + (u >= OUT_AT - 1)

        UNITS = ((0, 2), (2, 5), (5, 8), (8, 12))

        def live(j):
            return not isinstance(j, int) or 0 <= j < TILES

        def over_tiles(eng, tile):
            for j in range(4):
                tile(j, j // 2, j % 2)
            with eng.Fori(2, TILES // 2 - 1) as pair:
                for a in range(2):
                    tile(pair * 2 + a, pair, a)
            for j in range(TILES // 2 * 2 - 2, TILES + 2):
                tile(j, j // 2, j % 2)

        NLOOP = STEPS // 4

        @block.sync
        def _(sp):
            for n in range(4):
                sp.dma_start(acc[:, 4 * n:4 * n + 4, :],
                             x_rows[512 * n:512 * (n + 1), :].rearrange("(c p) d -> p c d", p=P))\
                  .then_inc(x_loaded[n], 16)
            sp.dma_start(wk_sb, wkT.rearrange("(k p) n -> p k n", p=P)).then_inc(proj_loaded, 16)
            sp.dma_start(wq_sb, wqT.rearrange("(k p) n -> p k n", p=P)).then_inc(proj_loaded, 16)
            sp.dma_start(wvr_sb[:, :, 0:DKV], wvT.rearrange("(k p) n -> p k n", p=P)).then_inc(proj_loaded, 16)
            sp.dma_start(wvr_sb[:, :, DKV:DKV + E], router_w.rearrange("(k p) n -> p k n", p=P)).then_inc(proj_loaded, 16)

            sp.dma_start(wg_sb, w_gate.rearrange("(k p) n -> p k n", p=P)).then_inc(shw_loaded, 16)
            sp.dma_start(wu_sb, w_up.rearrange("(k p) n -> p k n", p=P)).then_inc(shw_loaded, 16)
            sp.dma_start(wd_sb, w_down.rearrange("(k p) n -> p k n", p=P)).then_inc(shw_loaded, 16)
            sp.dma_start(mixw[:, 0:1], memory_weight.partition_broadcast(P)).then_inc(small_loaded, 16)
            sp.wait_ge(mem_zero, 1)
            for a in range(2):
                sp.dma_start(mem_w[DKV * a:DKV * (a + 1), MEMW * a:MEMW * a + DKV], memory).then_inc(mem_loaded, 16)
                sp.dma_start(mem_w[DKV * a:DKV * (a + 1), MEMW * a + DKV:MEMW * (a + 1)], memory_norm)\
                  .then_inc(mem_loaded, 16)
            sp.wait_ge(consts_ready, 1)
            sp.dma_start(slot_x.rearrange("(j p) d -> p j d", p=P),
                         zeros[:, :].unsqueeze(1).to_broadcast([P, TILES, D])).then_inc(slots_cleared, 16)
            for n in range(4):
                sp.dma_start(k_st[n][R:RM, :], ones[0:3, :]).then_inc(ones_rows, 16)
            for part, done in ((0, part_hi), (1, part_mid), (2, part_lo)):
                sp.wait_ge(done, 1)
                for c in range(NC):
                    if K_PART[c] == part:
                        sp.dma_start(k_stacks[:, DH * c:DH * (c + 1), :], kc[part][:, :]).then_inc(stacks_written, 16)
            for part, done in ((0, part_hi), (1, part_mid), (2, part_lo)):
                for m in range(KD):
                    sp.wait_ge(done, 2 + m)
                    for c in range(NC):
                        if Q_PART[c] == part:
                            sp.dma_start(q_stacks[2 * m:2 * m + 2, :, DH * c:DH * (c + 1), :], qc[part][:, m, :])\
                              .then_inc(stacks_written, 16)
            sp.wait_ge(stacks_written, 16 * NC * (1 + KD))

            def load_stack(b, h, n):
                sp.dma_start(q_st[n][0:R, :, :],
                             q_stacks[:, bass.ds(h, 1), :, bass.ds(b * SEQ, SEQ)].rearrange("g o r t -> r (o g) t"))\
                  .then_inc(stack_loaded[n], 16)
                sp.dma_start(k_st[n][0:R, :],
                             k_stacks[bass.ds(h, 1), :, bass.ds(b * SEQ, SEQ)].rearrange("o r t -> r (o t)"))\
                  .then_inc(stack_loaded[n], 16)

            def m_rows(i, s):
                sp.wait_ge(m_ready, i + 1)
                for c in range(3):
                    sp.dma_start(q_st[s % 4][R + c:R + c + 1, :, :].rearrange("o g s -> o (g s)"),
                                 m_parts[0:16, s % 2, c, :]).then_inc(m_loaded[s % 2], 16)

            sp.wait_ge(s_hused, 2 * NF)
            for n in range(3):
                load_stack(0, n, n)
            def steps(b, h0, last):
                for s in range(4):
                    i = b * H + (h0 + s)
                    m_rows(i, s)
                    if last and s > 0:
                        continue
                    wait(sp, scores_ready, i * 16)
                    if h0 == 4 and s > 0:
                        load_stack(b + 1, s - 1, (s + 3) % 4)
                    else:
                        load_stack(b, h0 + s + 3, (s + 3) % 4)
            steps(0, 0, False)
            steps(0, 4, False)
            with sp.Fori(1, BATCH - 1) as b:
                steps(b, 0, False)
                steps(b, 4, False)
            steps(BATCH - 1, 0, False)

            def load_x(j, a):
                wait(sp, exT_in_psum, j - 1)
                sp.dma_start(e_x[:, a, :], slot_x[bass.ds(j * P, P), :]).then_inc(ex_loaded[a], 16)

            sp.wait_ge(scattered, 16 * TOPK * NT)
            load_x(0, 0)
            load_x(1, 1)
            steps(BATCH - 1, 4, True)

            def store_y(j, a):
                sp.wait_ge(y_ready, j + 1)
                sp.dma_start(slot_y[bass.ds(j * P, P), :], e_y[:, a, :]).then_inc(y_stored[a], 16)

            def tile(j, pair, a):
                if live(j + 2):
                    load_x(j + 2, a)
                if live(j - 2):
                    store_y(j - 2, a)

            over_tiles(sp, tile)

            with sp.Fori(0, 4) as n:
                sp.wait_ge(s_mix, (n + 1) * 8)
                sp.dma_start(out_rows[bass.ds(n * 512, 512), :].rearrange("(c p) d -> p c d", p=P),
                             acc[:, bass.ds(n * 4, 4), :]).then_inc(stored, 16)
            sp.wait_ge(stored, 64)

        @block.gpsimd
        def _(pool):
            count = [0]

            def link(ins):
                count[0] += 1
                ins.then_inc(pool_step, 1)
                pool.wait_ge(pool_step, count[0])

            pool.memset(ident[:, :], 0.0).then_inc(ident_zero, 1)
            pool.wait_ge(ident_zero, 1)
            pool.affine_select(out=ident[:, :], in_=ident[:, :], compare_op=ALU.not_equal, fill=1.0,
                               base=0, pattern=[[-1, P]], channel_multiplier=1).then_inc(ident_ready, 1)
            pool.memset(mem_w[:, :], 0.0).then_inc(mem_zero, 1)
            pool.memset(zeros[:, :], 0.0)
            pool.memset(v_head[:, :, :, :], 0.0)
            link(pool.memset(ones[:, :], 1.0))
            pool.memset(v_head[:, :, :, DH:DH + 1], 1.0)
            pool.iota(iota_e[:, :], pattern=[[1, E]], base=0, channel_multiplier=0,
                      allow_small_or_imprecise_dtypes=True)
            pool.iota(iota_t[:, :], pattern=[[1, TILES]], base=0, channel_multiplier=0,
                      allow_small_or_imprecise_dtypes=True)
            pool.iota(full_at[:, :], pattern=[[P, NT]], base=0, channel_multiplier=0,
                      allow_small_or_imprecise_dtypes=True)
            pool.affine_select(out=before[:, :], in_=ones[:, 0:P], compare_op=ALU.is_gt, fill=0.0,
                               base=0, pattern=[[1, P]], channel_multiplier=-1).then_inc(consts_ready, 1)

            def scatter(first, count):
                for n in range(first, first + count):
                    pool.indirect_dma_start(
                        out=slot_x, out_offset=bass.IndirectOffsetOnAxis(ap=slot[:, n:n + 1], axis=0),
                        in_=xn[:, n % NT, :], in_offset=None).then_inc(scattered, 16)

            pool.wait_ge(vl_copied, 2)

            def stage_v(i, b, h, s):
                wait(pool, pv_done, ST * (i - 1))
                pool.tensor_copy(v_head[:, s % 2, :, 0:DH],
                                 v_all[:, bass.ds(b * ST, ST), bass.ds(h * DH, DH)]).then_inc(v_head_ready, 1)

            def split_m(i, s, pairs):
                a = s % 2
                pool.wait_ge(negm_ready, i + 1)
                wait(pool, m_loaded[a], pairs * 48)
                pool.tensor_tensor(m_parts[:, a, 0, :], negm[:, a, :], zeros[0:16, 0:P], ALU.subtract).then_inc(m_hi, 1)
                pool.wait_ge(m_hi, i + 1)
                pool.tensor_tensor(negr[:, a, :], negm[:, a, :], m_parts[:, a, 0, :], ALU.subtract).then_inc(m_res, 1)
                pool.wait_ge(m_res, i + 1)
                pool.tensor_tensor(m_parts[:, a, 1, :], negr[:, a, :], zeros[0:16, 0:P], ALU.subtract).then_inc(m_mid, 1)
                pool.wait_ge(m_mid, i + 1)
                pool.tensor_tensor(m_parts[:, a, 2, :], negr[:, a, :], m_parts[:, a, 1, :], ALU.subtract)\
                    .then_inc(m_ready, 1)

            def add_o(i, b, h, s):
                pool.wait_ge(o_ready, i + 1)
                place = acc[:, bass.ds(b * ST, ST), :].rearrange("p t (g c) -> p t g c", g=G)[
                    :, :, :, bass.ds(h * DH, DH)]
                pool.tensor_tensor(place, place, otmp[:, s % 2, :, :].rearrange("p (t g) d -> p t g d", t=ST),
                                   ALU.add).then_inc(o_added, 1)

            pool.wait_ge(s_add, 2 * 4)
            for c in range(NT):
                pool.wait_ge(mem_used, c + 1)
                pool.tensor_tensor(acc[:, c, :], acc[:, c, :], mtmp[:, c % 2, :], ALU.add).then_inc(mem_added, 1)
            pool.wait_ge(mem_added, NT)
            pool.wait_ge(routed, 1)
            pool.wait_ge(slots_cleared, 16)

            def steps(blk, b, h0, first=False):
                for s in range(4):
                    i = blk * 4 + s
                    stage_v(i, b, h0 + s, s)
                    split_m(i, s, blk * 2 + s // 2)
                    if isinstance(i, int) and i < 8:
                        scatter(4 * i, 4)
                    if first and s < 2:
                        continue
                    if s >= 2:
                        add_o(i - 2, b, h0 + s - 2, s)
                    elif h0 == 4:
                        add_o(i - 2, b, h0 + s - 2, s)
                    else:
                        add_o(i - 2, b - 1, H + s - 2, s)

            steps(0, 0, 0, first=True)
            steps(1, 0, 4)
            with pool.Fori(1, BATCH) as b:
                steps(b * 2, b, 0)
                steps(b * 2 + 1, b, 4)
            add_o(STEPS - 2, BATCH - 1, H - 2, 0)
            add_o(STEPS - 1, BATCH - 1, H - 1, 1)

            for a in range(2):
                pool.wait_ge(y_stored[a], 16 * ((TILES + 1 - a) // 2))
            for n in range(NT // 4):
                wait(pool, s_mix, 8 * (n - 1))
                for c in range(4):
                    for k in range(TOPK):
                        w = k * NT + 4 * n + c
                        pool.indirect_dma_start(
                            out=gath[:, n % 2, 2 * c + k, :], out_offset=None, in_=slot_y,
                            in_offset=bass.IndirectOffsetOnAxis(ap=slot[:, w:w + 1], axis=0)).then_inc(gathered[n % 2], 16)

        @block.scalar
        def _(act):
            def sqrt_var(n):
                act.wait_ge(var_ready, n + 1)
                act.activation(sd[:, 4 * n:4 * n + 4], meanvar[:, 4 * n:4 * n + 4, 1], ACT.Sqrt).then_inc(sd_ready, 1)

            def copy_xT(n):
                act.wait_ge(xT_in_psum, n + 1)
                act.activation(xnT[:, n % 2, 512 * (n // 2):512 * (n // 2 + 1)], ps[:, n % 4, :], ACT.Copy)\
                   .then_inc(xT_copied, 1)

            def copy_qk(u):
                n, part = divmod(u, 3)
                act.wait_ge(qk_in_psum, u + 1)
                if part == 0:
                    ins = act.activation(kf[:, 512 * n:512 * (n + 1)], ps[0:DKV, 4 + u % 4, :], ACT.Copy)
                else:
                    ins = act.activation(qf[:, part - 1, 512 * n:512 * (n + 1)], ps[:, 4 + u % 4, :], ACT.Copy)
                ins.then_inc(qk_copied, 1)

            for n in range(4):
                sqrt_var(n)
                copy_xT(2 * n)
                copy_xT(2 * n + 1)
                if n > 0:
                    for u in range(*UNITS[n - 1]):
                        copy_qk(u)
            for u in range(*UNITS[3]):
                copy_qk(u)
            act.wait_ge(qk_copied, 12)
            act.activation(kc[0], kf, ACT.Copy).then_inc(part_hi, 1)
            act.wait_ge(vl_in_psum, 1)
            act.activation(vl_all[:, 0:2 * VT, :].rearrange("p (a c) n -> p a (c n)", a=2), ps[:, 1:3, 0:VT * VW],
                           ACT.Copy).then_inc(vl_copied, 1)
            act.activation(vl_all[:, 2 * VT:NT, :].rearrange("p c n -> p (c n)"), ps[:, 3, 0:(NT - 2 * VT) * VW],
                           ACT.Copy).then_inc(vl_copied, 1)
            act.wait_ge(small_loaded, 16)
            act.activation(mixw[:, 1:2], mixw[:, 0:1], ACT.Exp, scale=-1.0).then_inc(mix_exp, 1)
            act.wait_ge(gap_ready, 1)
            act.activation(score[:, 1, :], score[:, 1, :], ACT.Exp).then_inc(gap_exp, 1)
            for m in range(KD):
                act.activation(qc[0][:, m, :], qf[:, m, :], ACT.Copy).then_inc(part_hi, 1)

            def silu_shared(n, f):
                act.wait_ge(s_up, n * (2 * NF) + (2 * f + 1))
                wait(act, s_h, n * NF + max(f - 1, 0))
                act.activation(sh_silu[:, f % 2, :], ps[:, f % 2, :], ACT.Silu).then_inc(s_silu, 1)

            def k_mid():
                act.wait_ge(residual, 1)
                act.activation(kc[1], kr, ACT.Copy).then_inc(part_mid, 1)

            def q_mid(m):
                act.wait_ge(residual, 2 + m)
                act.activation(qc[1][:, m, :], qr[:, m, :], ACT.Copy).then_inc(part_mid, 1)

            def q_tanh():
                act.wait_ge(q_elu_parts, 1)
                act.activation(qr, qr, ACT.Tanh, scale=0.5).then_inc(q_elu_parts, 1)

            def q_exp():
                act.wait_ge(q_min, 1)
                act.activation(qe, qr, ACT.Exp).then_inc(q_elu_parts, 1)

            between = {(0, 0): k_mid, (0, 2): lambda: q_mid(0), (0, 4): lambda: q_mid(1),
                       (0, 7): q_exp, (1, 0): q_tanh}
            for n in range(2):
                for f in range(NF):
                    silu_shared(n, f)
                    if (n, f) in between:
                        between[n, f]()

            def negate_max(i, s):
                act.wait_ge(maxT_in_psum, i + 1)
                wait(act, m_ready, i - 1)
                act.activation(negm[:, s % 2, :], ps[0:16, RING[MAX_AT % 3], 0:P], ACT.Copy, scale=-1.0)\
                   .then_inc(negm_ready, 1)

            def evacuate_o(i, s):
                act.wait_ge(pv_done, ST * (i + 1))
                wait(act, oT_in_psum, i - 1)
                act.activation(o_sb[:, s % 2, :], ps[:, 6, :], ACT.Copy).then_inc(o_copied, 1)

            def copy_oT(i, s):
                act.wait_ge(oT_in_psum, i + 1)
                wait(act, o_ready, i - 1)
                act.activation(oT_sb[:, s % 2, :, :],
                               ps[:, RING[OUT_AT % 3], :].rearrange("p (w n) -> p w n", n=32)[:, :, 0:DH + 1],
                               ACT.Copy).then_inc(oT_copied, 1)

            def exps(i, s, last=False):
                for u in range(16):
                    t, g = divmod(u, G)
                    if u == 4 and not last:
                        negate_max(i + 1, s + 1)
                    if not (isinstance(i, int) and i == 0):
                        if u == 6:
                            evacuate_o(i - 1, s + 1)
                        if u == 8:
                            copy_oT(i - 1, s + 1)
                    act.wait_ge(scores_ready, i * 16 + (u + 1))
                    if g == 0:
                        wait(act, pv_done, i * ST + (t - 1))
                    act.activation(probs[:, t % 2, g, :], ps[:, RING[turn_of(u) % 3], :], ACT.Exp, scale=SCALE)\
                       .then_inc(probs_ready, 1)

            def load_expert(n):
                act.dma_start(w1_sb[:, n, :, :], w1[n].rearrange("(k p) n -> p k n", p=P)).then_inc(w12_loaded, 16)
                act.dma_start(w2_sb[:, n, :, :], w2[n].rearrange("(k p) n -> p k n", p=P)).then_inc(w12_loaded, 16)

            act.wait_ge(mem_used, NT)
            act.wait_ge(stacks_written, 16 * NC * (1 + KD))
            negate_max(0, 0)
            for i in range(4):
                exps(i, i)
                load_expert(i)
            with act.Fori(1, NLOOP - 1) as blk:
                for s in range(4):
                    exps(blk * 4 + s, s)
            for i in range(STEPS - 4, STEPS):
                load_expert(i - (STEPS - 8))
                exps(i, i % 4, last=i == STEPS - 1)
            evacuate_o(STEPS - 1, 1)
            copy_oT(STEPS - 1, 1)

            act.wait_ge(scattered, 16 * TOPK * NT)

            def copy_xT(j, a):
                act.wait_ge(exT_in_psum, j + 1)
                wait(act, up_done, (j - 1) * 2)
                act.activation(e_xT[:, a, :, :], ps[:, 4, 0:D].rearrange("p (k n) -> p k n", k=KD), ACT.Copy)\
                   .then_inc(exT_ready, 1)

            def silu_g(j, a):
                act.wait_ge(up_done, j * 2 + 1)
                wait(act, h_ready, j - 1)
                act.activation(e_silu[:, a, :], ps[:, 2 * a, :], ACT.Silu).then_inc(silu_done, 1)

            def copy_y(j, pair, a):
                act.wait_ge(y_in_psum, j + 1)
                wait(act, y_stored[a], pair * 16)
                act.activation(e_y[:, a, :], ps[:, 6 + a, 0:D], ACT.Copy).then_inc(y_ready, 1)

            def tile(j, pair, a):
                if live(j):
                    silu_g(j, a)
                if live(j + 1):
                    copy_xT(j + 1, 1 - a)
                if live(j - 2):
                    copy_y(j - 2, pair - 1, a)
                if isinstance(j, int) and j == 3:
                    load_shared()

            def load_shared():
                act.wait_ge(pv_done, ST * STEPS)
                act.dma_start(wg_sb, w_gate.rearrange("(k p) n -> p k n", p=P)).then_inc(shw_loaded, 16)
                act.dma_start(wu_sb, w_up.rearrange("(k p) n -> p k n", p=P)).then_inc(shw_loaded, 16)
                act.dma_start(wd_sb, w_down.rearrange("(k p) n -> p k n", p=P)).then_inc(shw_loaded, 16)

            copy_xT(0, 0)
            over_tiles(act, tile)

            with act.Fori(2, NT // 4) as n:
                for f in range(NF):
                    silu_shared(n, f)

        @block.vector
        def _(dve):
            count = [0]

            def link(ins):
                count[0] += 1
                ins.then_inc(dve_step, 1)
                dve.wait_ge(dve_step, count[0])

            for n in range(4):
                tiles = range(4 * n, 4 * n + 4)
                part = slice(4 * n, 4 * n + 4)
                dve.wait_ge(x_loaded[n], 16)
                for c in tiles:
                    last = dve.bn_stats(stats[:, c, :], acc[:, c, :])
                link(last)
                for c in tiles:
                    last = dve.bn_aggr(meanvar[:, c, :], stats[:, c, :])
                link(last)
                dve.tensor_scalar_add(meanvar[:, part, 1], meanvar[:, part, 1], EPS).then_inc(var_ready, 1)
                dve.wait_ge(sd_ready, n + 1)
                link(dve.reciprocal(rstd[:, part], sd[:, part]))
                link(dve.tensor_tensor(sd[:, part], rstd[:, part], rstd[:, part], ALU.mult))
                link(dve.tensor_tensor(sd[:, part], sd[:, part], meanvar[:, part, 1], ALU.mult))
                link(dve.tensor_scalar(sd[:, part], sd[:, part], -0.5, 1.5, ALU.mult, ALU.add))
                link(dve.tensor_tensor(rstd[:, part], rstd[:, part], sd[:, part], ALU.mult))
                for c in tiles:
                    dve.tensor_scalar(xn[:, c, :], acc[:, c, :], meanvar[:, c, 0:1], rstd[:, c:c + 1],
                                      ALU.subtract, ALU.mult).then_inc(xn_ready, 1)

            dve.wait_ge(vl_copied, 2)
            for c in range(NT):
                last = dve.max(top[:, c, :], logits[:, c, :])
            link(last)
            for c in range(NT):
                last = dve.max_index(topi[:, c, :], top[:, c, :], logits[:, c, :])
            link(last)
            dve.tensor_tensor(score[:, 1, :], top[:, :, 1], top[:, :, 0], ALU.subtract).then_inc(gap_ready, 1)
            link(dve.tensor_copy(choice[:, :, :], topi[:, :, 0:TOPK].rearrange("p c k -> p k c")))
            dve.wait_ge(consts_ready, 1)
            W = TOPK * NT
            dve.tensor_tensor(onehot[:, :, :],
                              choice[:, :, :].rearrange("p k c -> p (k c)").unsqueeze(2).to_broadcast([P, W, E]),
                              iota_e[:, :].unsqueeze(1).to_broadcast([P, W, E]), ALU.is_equal)\
               .then_inc(onehot_ready, 1)

            def res(n, f, r, c):
                dve.wait_ge(part_hi, n)
                dve.tensor_tensor(r, f, c, ALU.subtract).then_inc(residual, 1)

            def low(n, r, c, out_part):
                dve.wait_ge(part_mid, n)
                dve.wait_ge(residual, n)
                dve.tensor_tensor(out_part, r, c, ALU.subtract).then_inc(part_lo, 1)

            def elu_min():
                dve.wait_ge(part_lo, 3)
                dve.tensor_scalar_min(qr, qf, 0.0).then_inc(q_min, 1)

            def elu_mult(m):
                dve.wait_ge(q_elu_parts, 2)
                link(dve.scalar_tensor_tensor(qr[:, m, :], qe[:, m, :], 1.0, qr[:, m, :], ALU.add, ALU.mult))

            def elu_add(m):
                dve.scalar_tensor_tensor(qf[:, m, :], qf[:, m, :], 0.0, qr[:, m, :], ALU.max, ALU.add)\
                   .then_inc(sigma_ready, 1)

            def copy_ranks():
                dve.wait_ge(ranks_in_psum, 1)
                dve.tensor_copy(rank[:, :, :].rearrange("p w e -> p (w e)"), ps[:, 0, 0:W * E])
                ins = dve.tensor_copy(total[:, :, :].rearrange("p w e -> p (w e)"), ps[:, 0, W * E:2 * W * E])
                ins.then_inc(ranks_copied, 1)
                dve.wait_ge(ranks_copied, 1)

            chunk_sum, chunk_tmp = run_a, run_b
            expert_sum, expert_tmp = cum_a, cum_b

            def sum_chunks():
                src, dst, other = total, run_a, run_b
                step = 1
                while step < W:
                    dve.tensor_copy(dst[:, 0:step, :], src[:, 0:step, :])
                    link(dve.tensor_tensor(dst[:, step:W, :], src[:, step:W, :], src[:, 0:W - step, :], ALU.add))
                    src, dst, other = dst, other, dst
                    step *= 2
                assert src is chunk_sum

            def count_tiles():
                link(dve.tensor_tensor(gt, chunk_sum[:, W - 1, :].unsqueeze(2).to_broadcast([P, E, NT]),
                                       full_at[:, :].unsqueeze(1).to_broadcast([P, E, NT]), ALU.is_gt))
                link(dve.tensor_reduce(tiles_e[:, :], gt, X_AXIS, ALU.add))
                csrc, cdst, cother = tiles_e, cum_a, cum_b
                step = 1
                while step < E:
                    dve.tensor_copy(cdst[:, 0:step], csrc[:, 0:step])
                    link(dve.tensor_tensor(cdst[:, step:E], csrc[:, step:E], csrc[:, 0:E - step], ALU.add))
                    csrc, cdst, cother = cdst, cother, cdst
                    step *= 2
                assert csrc is expert_sum
                link(dve.tensor_tensor(le, expert_sum[:, :].unsqueeze(1).to_broadcast([P, TILES, E]),
                                       iota_t[:, :].unsqueeze(2).to_broadcast([P, TILES, E]), ALU.is_le))
                link(dve.tensor_reduce(expert_f[:, :], le, X_AXIS, ALU.add))
                dve.tensor_scalar_min(expert[:, :], expert_f[:, :], float(E - 1)).then_inc(experts_known, 1)

            def find_slots():
                link(dve.tensor_tensor(expert_tmp[:, :], expert_sum[:, :], tiles_e[:, :], ALU.subtract))
                link(dve.tensor_tensor(chunk_tmp, chunk_sum, total, ALU.subtract))
                link(dve.tensor_tensor(rank, rank, chunk_tmp, ALU.add))
                link(dve.scalar_tensor_tensor(chunk_tmp, expert_tmp[:, :].unsqueeze(1).to_broadcast([P, W, E]),
                                              float(P), rank, ALU.mult, ALU.add))
                link(dve.tensor_tensor(rank, chunk_tmp, onehot[:, :, :], ALU.mult))
                link(dve.tensor_reduce(slot_f[:, :], rank, X_AXIS, ALU.add))
                dve.tensor_copy(slot[:, :], slot_f[:, :]).then_inc(routed, 1)

            def weights_of_terms():
                dve.wait_ge(gap_exp, 1)
                link(dve.tensor_scalar_add(score[:, 0, :], score[:, 1, :], 1.0))
                link(dve.reciprocal(score[:, 0, :], score[:, 0, :]))
                dve.tensor_tensor(score[:, 1, :], score[:, 1, :], score[:, 0, :], ALU.mult)
                dve.wait_ge(mix_exp, 1)
                link(dve.tensor_scalar_add(mixw[:, 2:3], mixw[:, 1:2], 1.0))
                link(dve.reciprocal(mixw[:, 2:3], mixw[:, 2:3]))
                link(dve.tensor_scalar(mixw[:, 3:4], mixw[:, 2:3], -1.0, 1.0, ALU.mult, ALU.add))

            def shared_h(n, f):
                dve.wait_ge(s_silu, n * NF + (f + 1))
                dve.wait_ge(s_up, n * (2 * NF) + (2 * f + 2))
                wait(dve, s_hused, n * NF + max(f - 1, 0))
                dve.tensor_tensor(sh_h[:, f % 2, :], sh_silu[:, f % 2, :], ps[:, 2 + f % 2, :], ALU.mult)\
                   .then_inc(s_h, 1)

            def row_of(c):
                return acc[:, bass.ds(c, 1), :].rearrange("p o d -> p (o d)")

            def add_shared(n):
                dve.wait_ge(s_hused, n * NF + NF)
                for c in range(4):
                    row = row_of(n * 4 + c)
                    dve.tensor_tensor(row, row, ps[:, 4 + c, 0:D], ALU.add).then_inc(s_add, 1)

            res(1, kf, kr, kc[0])
            res(2, qf[:, 0, :], qr[:, 0, :], qc[0][:, 0, :])
            between = {
                (0, 0): lambda: (low(1, kr, kc[1], kc[2]), res(3, qf[:, 1, :], qr[:, 1, :], qc[0][:, 1, :])),
                (0, 2): lambda: low(2, qr[:, 0, :], qc[1][:, 0, :], qc[2][:, 0, :]),
                (0, 4): lambda: low(3, qr[:, 1, :], qc[1][:, 1, :], qc[2][:, 1, :]),
                (0, 5): elu_min,
                (0, 6): weights_of_terms,
                (1, 0): sum_chunks,
                (1, 1): count_tiles,
                (1, 2): find_slots,
                (1, 3): lambda: (elu_mult(0), elu_add(0)),
                (1, 4): lambda: (elu_mult(1), elu_add(1)),
            }
            for n in range(2):
                for f in range(NF):
                    shared_h(n, f)
                    if (n, f) in between:
                        between[n, f]()
                add_shared(n)
                if n == 0:
                    copy_ranks()
            dve.wait_ge(s_add, 2 * 4)
            for c in range(NT):
                dve.wait_ge(mem_in_psum, c + 1)
                read = ps[:, c % 4, 0:G * MEMW].rearrange("p (g n) -> p g n", g=G)
                link(dve.reciprocal(mden[:, c % 2, :], read[:, :, DKV]))
                wait(dve, mem_added, c - 1)
                dve.scalar_tensor_tensor(
                    mtmp[:, c % 2, :].rearrange("p (g n) -> p g n", g=G), read[:, :, 0:DKV], mixw[:, 2:3],
                    mden[:, c % 2, :].unsqueeze(2).to_broadcast([P, G, DKV]), ALU.mult, ALU.mult)\
                   .then_inc(mem_used, 1)

            def maxima(i, s, u):
                dve.wait_ge(a_ready, i * 16 + (u + 1))
                if u == 0:
                    wait(dve, maxT_in_psum, i - 1)
                dve.reduce_max(smax[:, s % 2, u:u + 1], ps[:, u % 4, :], X_AXIS).then_inc(max_done, 1)

            def finish_o(i, s):
                a = s % 2
                dve.wait_ge(oT_copied, i + 1)
                wait(dve, o_added, i - 1)
                o = oT_sb[:, a, :, :]
                dve.reciprocal(rden[:, a, :], o[:, :, DH]).then_inc(rden_ready, 1)
                dve.wait_ge(rden_ready, i + 1)
                dve.scalar_tensor_tensor(otmp[:, a, :, :], o[:, :, 0:DH], mixw[:, 3:4],
                                         rden[:, a, :].unsqueeze(2).to_broadcast([P, 16, DH]), ALU.mult, ALU.mult)\
                   .then_inc(o_ready, 1)

            def step(i, s, first=False, ahead=True):
                for u in range(16):
                    if u == 13 and not first:
                        finish_o(i - 1, s + 1)
                    if ahead:
                        maxima(i + 2, s, u)

            for i in range(2):
                for u in range(16):
                    maxima(i, i, u)
            for i in range(4):
                step(i, i, first=i == 0)
            with dve.Fori(1, NLOOP - 1) as blk:
                for s in range(4):
                    step(blk * 4 + s, s)
            for i in range(STEPS - 4, STEPS):
                step(i, i % 4, ahead=i + 2 < STEPS)
            finish_o(STEPS - 1, STEPS - 1)

            def copy_hT(j, a):
                dve.wait_ge(hT_in_psum, j + 1)
                wait(dve, y_in_psum, j - 1)
                dve.tensor_copy(e_hT[:, a, :, :].rearrange("p k n -> p (k n)"), ps[:, 5, :]).then_inc(hT_ready, 1)

            def make_h(j, a):
                dve.wait_ge(silu_done, j + 1)
                dve.wait_ge(up_done, j * 2 + 2)
                wait(dve, hT_in_psum, j - 1)
                dve.tensor_tensor(e_h[:, a, :], e_silu[:, a, :], ps[:, 2 * a + 1, :], ALU.mult).then_inc(h_ready, 1)

            def tile(j, pair, a):
                if live(j - 1):
                    copy_hT(j - 1, 1 - a)
                if live(j):
                    make_h(j, a)

            over_tiles(dve, tile)

            dve.wait_ge(o_added, STEPS)

            def mix(batch, half, n):
                dve.wait_ge(gathered[half], n * (16 * 8) + 16 * 8)
                for k in range(TOPK):
                    for c in range(4):
                        row = row_of(batch * 4 + c)
                        if k == 1:
                            dve.wait_ge(s_mix, batch * 8 + (c + 1))
                        dve.scalar_tensor_tensor(row, gath[:, half, 2 * c + k, :],
                                                 score[:, k, bass.ds(batch * 4 + c, 1)], row,
                                                 ALU.mult, ALU.add).then_inc(s_mix, 1)

            with dve.Fori(0, 2) as n:
                for f in range(NF):
                    shared_h(n + 2, f)
                    if f == 5:
                        dve.wait_ge(s_add, n * 4 + 8)
                        mix(n * 2, 0, n)
                add_shared(n + 2)
                dve.wait_ge(s_add, n * 4 + 12)
                mix(n * 2 + 1, 1, n)

        @block.tensor
        def _(pe):
            pe.wait_ge(ident_ready, 1)

            def transpose_xn(n):
                m, g = n % 2, n // 2
                pe.wait_ge(xn_ready, 4 * g + 4)
                if n >= 4:
                    pe.wait_ge(xT_copied, n - 3)
                for c in range(4):
                    last = pe.transpose(ps[:, n % 4, P * c:P * (c + 1)], xn[:, 4 * g + c, P * m:P * (m + 1)],
                                        ident[:, :])
                last.then_inc(xT_in_psum, 1)

            def project_qk(u):
                n, part = divmod(u, 3)
                pe.wait_ge(xT_copied, 2 * n + 2)
                wait(pe, qk_copied, u - 3)
                for k in range(KD):
                    tokens = xnT[:, k, 512 * n:512 * (n + 1)]
                    if part == 0:
                        last = pe.matmul(ps[0:DKV, 4 + u % 4, :], wk_sb[:, k, :], tokens,
                                         start=k == 0, stop=k == KD - 1)
                    else:
                        last = pe.matmul(ps[:, 4 + u % 4, :], wq_sb[:, k, P * (part - 1):P * part], tokens,
                                         start=k == 0, stop=k == KD - 1)
                last.then_inc(qk_in_psum, 1)

            for n in range(4):
                transpose_xn(2 * n)
                transpose_xn(2 * n + 1)
                if n == 0:
                    pe.wait_ge(proj_loaded, 64)
                for u in range(*UNITS[n]):
                    project_qk(u)
            for c in range(NT):
                for k in range(KD):
                    last = pe.matmul(ps[:, 1 + c // VT, VW * (c % VT):VW * (c % VT + 1)],
                                     xnT[:, k, P * c:P * (c + 1)], wvr_sb[:, k, :], start=k == 0, stop=k == KD - 1)
            last.then_inc(vl_in_psum, 1)

            def shared_down(n, f):
                pe.wait_ge(s_h, n * NF + (f + 1))
                if f == 0:
                    wait(pe, s_add, n * 4)
                for c in range(4):
                    last = pe.matmul(ps[:, 4 + c, 0:D], sh_h[:, f % 2, P * c:P * (c + 1)], wd_sb[:, f, :],
                                     start=f == 0, stop=f == NF - 1)
                last.then_inc(s_hused, 1)

            def shared_group(n):
                for f in range(NF):
                    wait(pe, s_h, n * NF + max(f - 1, 0))
                    for w, bank in ((wg_sb, f % 2), (wu_sb, 2 + f % 2)):
                        for k in range(KD):
                            last = pe.matmul(ps[:, bank, :], w[:, k, P * f:P * (f + 1)],
                                             xnT[:, k, bass.ds(n * 512, 512)], start=k == 0, stop=k == KD - 1)
                        last.then_inc(s_up, 1)
                    if f > 0:
                        shared_down(n, f - 1)
                shared_down(n, NF - 1)

            pe.wait_ge(shw_loaded, 48)
            pe.wait_ge(vl_copied, 2)
            pe.wait_ge(qk_copied, 12)
            shared_group(0)
            pe.wait_ge(onehot_ready, 1)
            pe.wait_ge(s_h, NF)
            W = TOPK * NT
            flags = onehot[:, :, :].rearrange("p w e -> p (w e)")
            pe.matmul(ps[:, 0, 0:W * E], before[:, :], flags, start=True, stop=True)
            pe.matmul(ps[:, 0, W * E:2 * W * E], ones[:, 0:P], flags, start=True, stop=True)\
              .then_inc(ranks_in_psum, 1)
            pe.wait_ge(ranks_copied, 1)
            shared_group(1)
            pe.wait_ge(mem_loaded, 64)
            pe.wait_ge(sigma_ready, KD)
            pe.wait_ge(s_h, 2 * NF)
            for c in range(NT):
                wait(pe, mem_used, c - 3)
                for m in range(KD):
                    last = pe.matmul(ps[:, c % 4, 2 * MEMW * m:2 * MEMW * (m + 1)], qf[:, m, P * c:P * (c + 1)],
                                     mem_w[:, :], start=True, stop=True)
                last.then_inc(mem_in_psum, 1)

            pe.wait_ge(mem_used, NT)
            pe.wait_ge(s_add, 2 * 4)
            pe.wait_ge(ones_rows, 64)

            def bank_free(i, turn):
                back = turn - 3
                if back < 0:
                    back, i = back + TURNS, i - 1
                if back == MAX_AT:
                    wait(pe, negm_ready, i + 2)
                elif back == OUT_AT:
                    wait(pe, oT_copied, i)
                else:
                    v = back - (back > MAX_AT) - (back > OUT_AT)
                    wait(pe, probs_ready, i * 16 + (v + 1))

            def scores_for_max(i, s, blk, u):
                if u == 0:
                    pe.wait_ge(stack_loaded[s], blk * 32 + 32)
                wait(pe, max_done, i * 16 + (u - 3))
                g, st = divmod(u, ST)
                pe.matmul(ps[:, u % 4, :], q_st[s][0:R, g, P * st:P * (st + 1)], k_st[s][0:R, :],
                          start=True, stop=True).then_inc(a_ready, 1)

            def transpose_max(i, s):
                pe.wait_ge(max_done, i * 16 + 16)
                bank_free(i - 1, MAX_AT)
                pe.transpose(ps[0:16, RING[MAX_AT % 3], 0:P], smax[:, s % 2, :], ident[:, :])\
                  .then_inc(maxT_in_psum, 1)

            def transpose_o(i, s):
                pe.wait_ge(o_copied, i + 1)
                if isinstance(i, int) and i == STEPS - 1:
                    pe.wait_ge(probs_ready, STEPS * 16)
                else:
                    bank_free(i + 1, OUT_AT)
                for st in range(ST):
                    last = pe.transpose(ps[:, RING[OUT_AT % 3], P * st:P * (st + 1)],
                                        o_sb[:, s % 2, P * st:P * (st + 1)], ident[:, :])
                last.then_inc(oT_in_psum, 1)

            def weighted_values(i, s, t):
                pe.wait_ge(probs_ready, i * 16 + 4 * (t + 1))
                if t == 0:
                    pe.wait_ge(v_head_ready, i + 1)
                    wait(pe, o_copied, i)
                for g in range(G):
                    last = pe.matmul(ps[32 * g:32 * (g + 1), 6, :], v_head[:, s % 2, t, :], probs[:, t % 2, g, :],
                                     start=t == 0, stop=t == ST - 1)
                last.then_inc(pv_done, 1)

            def step(i, s, blk, first=False, ahead=True, last=False):
                pe.wait_ge(m_loaded[s % 2], blk * 96 + 48 * (s // 2 + 1))
                for t in range(ST):
                    for g in range(G):
                        u = G * t + g
                        if not (last and turn_of(u) - 3 == MAX_AT):
                            bank_free(i, turn_of(u))
                        pe.matmul(ps[:, RING[turn_of(u) % 3], :], k_st[s][0:RM, P * t:P * (t + 1)],
                                  q_st[s][0:RM, g, :], start=True, stop=True).then_inc(scores_ready, 1)
                        if ahead:
                            scores_for_max(i + 2, (s + 2) % 4, blk + (s + 2) // 4, u)
                    if t == MAX_AT // G - 1 and not last:
                        transpose_max(i + 1, s + 1)
                    if t == OUT_AT // G - 1 and not first:
                        transpose_o(i - 1, s + 1)
                    if t > 0:
                        weighted_values(i, s, t - 1)
                    elif not first:
                        weighted_values(i - 1, s + 3, ST - 1)

            for i in range(2):
                for u in range(16):
                    scores_for_max(i, i, 0, u)
                    if i == 1 and u == 3:
                        transpose_max(0, 0)
            for i in range(4):
                step(i, i, 0, first=i == 0)
            with pe.Fori(1, NLOOP - 1) as blk:
                for s in range(4):
                    step(blk * 4 + s, s, blk)
            for i in range(STEPS - 4, STEPS):
                step(i, i % 4, NLOOP - 1, ahead=i + 2 < STEPS, last=i == STEPS - 1)
            weighted_values(STEPS - 1, STEPS - 1, ST - 1)
            def transpose_x(j, pair, a):
                pe.wait_ge(ex_loaded[a], pair * 16 + 16)
                wait(pe, exT_ready, j)
                for k in range(KD):
                    last = pe.transpose(ps[:, 4, P * k:P * (k + 1)], e_x[:, a, P * k:P * (k + 1)], ident[:, :])
                last.then_inc(exT_in_psum, 1)

            def up(j, a):
                e = pe.value_load(expert[0:1, bass.ds(j, 1)], min_val=0, max_val=E - 1)
                pe.wait_ge(exT_ready, j + 1)
                wait(pe, h_ready, j - 1)
                for n in range(2):
                    for k in range(KD):
                        w = w1_sb[:, bass.ds(e, 1), k, F * n:F * (n + 1)].rearrange("p o n -> p (o n)")
                        last = pe.matmul(ps[:, 2 * a + n, :], e_xT[:, a, k, :], w, start=k == 0, stop=k == KD - 1)
                    last.then_inc(up_done, 1)

            def transpose_h(j, a):
                pe.wait_ge(h_ready, j + 1)
                wait(pe, hT_ready, j)
                for k in range(F // P):
                    last = pe.transpose(ps[:, 5, P * k:P * (k + 1)], e_h[:, a, P * k:P * (k + 1)], ident[:, :])
                last.then_inc(hT_in_psum, 1)

            def down(j, a):
                e = pe.value_load(expert[0:1, bass.ds(j, 1)], min_val=0, max_val=E - 1)
                pe.wait_ge(hT_ready, j + 1)
                wait(pe, y_ready, j - 1)
                for k in range(F // P):
                    w = w2_sb[:, bass.ds(e, 1), k, :].rearrange("p o n -> p (o n)")
                    last = pe.matmul(ps[:, 6 + a, 0:D], e_hT[:, a, k, :], w, start=k == 0, stop=k == F // P - 1)
                last.then_inc(y_in_psum, 1)

            def tile(j, pair, a):
                if live(j):
                    up(j, a)
                if live(j - 1):
                    transpose_h(j - 1, 1 - a)
                if live(j + 1):
                    transpose_x(j + 1, pair + a, 1 - a)
                if live(j - 2):
                    down(j - 2, a)

            pe.wait_ge(experts_known, 1)
            pe.wait_ge(probs_ready, 16 * STEPS)
            transpose_o(STEPS - 1, STEPS - 1)
            pe.wait_ge(oT_copied, STEPS)
            transpose_x(0, 0, 0)
            pe.wait_ge(w12_loaded, 16 * 2 * E)
            over_tiles(pe, tile)

            pe.wait_ge(shw_loaded, 96)
            pe.wait_ge(y_ready, TILES)
            with pe.Fori(2, NT // 4) as n:
                shared_group(n)


def kernel(L0_attn_x, L0_attn_Wq, L0_attn_Wk, L0_attn_Wv, L0_attn_memory, L0_attn_memory_norm, L0_attn_memory_weight,
           L0_ffn_router_w, L0_ffn_w1, L0_ffn_w2, L0_ffn_w_gate, L0_ffn_w_up, L0_ffn_w_down):
    import concourse.bacc as bacc
    from concourse.bass_utils import run_bass_kernel_spmd

    arrays = {
        "x": L0_attn_x, "wqT": np.asarray(L0_attn_Wq).T, "wkT": np.asarray(L0_attn_Wk).T,
        "wvT": np.asarray(L0_attn_Wv).T, "memory": L0_attn_memory, "memory_norm": L0_attn_memory_norm,
        "memory_weight": L0_attn_memory_weight, "router_w": L0_ffn_router_w, "w1": L0_ffn_w1, "w2": L0_ffn_w2,
        "w_gate": L0_ffn_w_gate, "w_up": L0_ffn_w_up, "w_down": L0_ffn_w_down,
    }
    arrays = {name: np.ascontiguousarray(a) for name, a in arrays.items()}
    nc = bacc.Bacc("TRN2", target_bir_lowering=False, num_devices=1)
    args = [nc.dram_tensor(name, a.shape, mybir.dt.from_np(a.dtype), kind="ExternalInput").ap()
            for name, a in arrays.items()]
    out = nc.dram_tensor("out", arrays["x"].shape, F32, kind="ExternalOutput").ap()
    build(nc, *args, out)
    result = run_bass_kernel_spmd(nc, [arrays], core_ids=[0])
    return result.results[0]["out"]
```

```python
from contextlib import ExitStack

import numpy as np

import concourse.bass as bass
from concourse import mybir

F32 = mybir.dt.float32
BF16 = mybir.dt.bfloat16
F32R = mybir.dt.float32r
I32 = mybir.dt.int32
U32 = mybir.dt.uint32
ALU = mybir.AluOpType
ACT = mybir.ActivationFunctionType
X_AXIS = mybir.AxisListType.X

P = 128


def wait(eng, sem, value):
    if isinstance(value, int) and value <= 0:
        return
    eng.wait_ge(sem, value)


def build(nc, x, wqT, wkT, wvT, memory, memory_norm, memory_weight, router_w, w1, w2, w_gate, w_up, w_down, out):
    BATCH, SEQ, D = x.shape
    T = BATCH * SEQ
    NT = T // P
    KD = D // P
    DKV = wkT.shape[1]
    DH = 8
    H = DKV // DH
    G = D // DKV
    ST = SEQ // P
    STEPS = BATCH * H
    E, _, F2 = w1.shape
    F = F2 // 2
    FS = w_gate.shape[1]
    TOPK = 2
    TILES = (T * TOPK + E * (P - 1)) // P
    SLOTS = TILES * P
    SCALE = float(np.float32(1.0 / np.sqrt(np.float32(DH))))
    EPS = 1e-5
    Q_PART = (0, 0, 0, 1, 1, 1, 2, 2, 2)
    K_PART = (0, 1, 2, 0, 1, 2, 0, 1, 2)
    NC = len(Q_PART)
    R = NC * DH
    RM = R + 3
    MEMW = DKV + 1
    assert (D, DKV, H, G, ST, E, F, FS, TILES) == (256, 64, 8, 4, 4, 8, 512, 1024, 39)

    q_stacks = nc.dram_tensor("q_stacks", [G, H, R, T], BF16, kind="Internal").ap()
    k_stacks = nc.dram_tensor("k_stacks", [H, R, T], BF16, kind="Internal").ap()
    slot_x = nc.dram_tensor("slot_x", [SLOTS, D], F32, kind="Internal").ap()
    slot_y = nc.dram_tensor("slot_y", [SLOTS, D], F32, kind="Internal").ap()

    x_rows = x.rearrange("b s d -> (b s) d")
    out_rows = out.rearrange("b s d -> (b s) d")

    with ExitStack() as ctx:
        def sb(name, shape, dt=F32):
            return ctx.enter_context(nc.sbuf_tensor(name, shape, dt))

        def sem(name):
            return ctx.enter_context(nc.semaphore(name))

        ps = ctx.enter_context(nc.psum_tensor("ps", [P, 8, 512], F32))

        acc = sb("acc", [P, NT, D])
        xn = sb("xn", [P, NT, D])
        xnT = sb("xnT", [P, KD, T])
        with nc.sbuf_tensor("split", [P, 24576], F32R) as split:
            pass
        big = sb("big", [P, 24576])
        att = sb("att", [P, 9216])
        o_sb = sb("o_sb", [P, 2, 512])
        v_all = sb("v_all", [P, NT, DKV])
        logits = sb("logits", [P, NT, E])
        router = sb("router", [P, KD, 32])
        v_head = sb("v_head", [P, 2, ST, 32])
        ident = sb("ident", [P, P])
        before = sb("before", [P, P], BF16)
        ones = sb("ones", [P, 512], BF16)
        zeros = sb("zeros", [P, D])
        mem_w = sb("mem_w", [P, 2 * MEMW])
        mixw = sb("mixw", [P, 4])
        stats = sb("stats", [P, NT, 6])
        meanvar = sb("meanvar", [P, NT, 2])
        sd = sb("sd", [P, NT])
        rstd = sb("rstd", [P, NT])
        top = sb("top", [P, NT, 8])
        topi = sb("topi", [P, NT, 8], U32)
        choice = sb("choice", [P, TOPK, NT])
        score = sb("score", [P, TOPK, NT])
        iota_e = sb("iota_e", [P, E])
        iota_t = sb("iota_t", [P, TILES])
        full_at = sb("full_at", [P, NT])
        onehot = sb("onehot", [P, TOPK * NT, E], BF16)
        tiles_e = sb("tiles_e", [P, E])
        cum_a = sb("cum_a", [P, E])
        cum_b = sb("cum_b", [P, E])
        slot_f = sb("slot_f", [P, TOPK * NT])
        slot = sb("slot", [P, TOPK * NT], U32)
        expert_f = sb("expert_f", [P, TILES])
        expert = sb("expert", [P, TILES], I32)
        mden = sb("mden", [P, 2, 2, G])
        smax = sb("smax", [P, 2, 16])
        negm = sb("negm", [16, 2, P])
        negr = sb("negr", [16, 2, P])
        m_parts = sb("m_parts", [16, 2, 3, P], BF16)
        rden = sb("rden", [P, 2, 32])
        oT_sb = sb("oT_sb", [P, 2, 32, DH + 1])
        otmp = sb("otmp", [P, 2, 32, DH])
        e_x = sb("e_x", [P, 2, D])

        rank, total, run_a, run_b = [big[:, 22288 + 256 * n:22544 + 256 * n].rearrange("p (w e) -> p w e", e=E)
                                     for n in range(4)]
        gt = big[:, 23312:23440].rearrange("p (e c) -> p e c", e=E)
        le = big[:, 23440:23440 + TILES * E].rearrange("p (j e) -> p j e", e=E)
        qf = big[:, 0:4096].rearrange("p (m t) -> p m t", m=KD)
        qr = big[:, 4096:8192].rearrange("p (m t) -> p m t", m=KD)
        qc = [big[:, 8192 + 2048 * n:8192 + 2048 * (n + 1)].bitcast(BF16).rearrange("p (m t) -> p m t", m=KD)
              for n in range(3)]
        kv = big[:, 14336:16384]
        kf = kv[0:DKV, :]
        kr = big[0:DKV, 16384:18432]
        qe = big[:, 14336:18432].rearrange("p (m t) -> p m t", m=KD)
        kc = [big[0:DKV, 18432 + 1024 * n:18432 + 1024 * (n + 1)].bitcast(BF16) for n in range(3)]
        wq_sb = big[:, 21504:22016].rearrange("p (k n) -> p k n", k=KD)
        wkv_sb = big[:, 22016:22272].rearrange("p (k n) -> p k n", k=KD)
        mtmp = big[:, 4096:6144].rearrange("p (a d) -> p a d", a=8)
        w1_sb = big[:, 0:16384].rearrange("p (e k n) -> p e k n", e=E, k=KD)
        w2_sb = big[:, 16384:24576].rearrange("p (e k n) -> p e k n", e=E, k=F // P)
        probs = att[:, 0:4096].rearrange("p (a g s) -> p a g s", a=2, g=G)
        q_st = [att[:, c:c + 1024].bitcast(BF16).rearrange("p (g s) -> p g s", g=G) for c in (6144, 7168, 4096, 5120)]
        k_st = [att[:, 8192 + 256 * n:8448 + 256 * n].bitcast(BF16) for n in range(4)]
        wg_sb = att[:, 0:2048].rearrange("p (k n) -> p k n", k=KD)
        wu_sb = att[:, 2048:4096].rearrange("p (k n) -> p k n", k=KD)
        wd_sb = att[:, 4096:6144].rearrange("p (k n) -> p k n", k=FS // P)
        sh_silu = att[:, 6144:7168].rearrange("p (a n) -> p a n", a=2)
        sh_h = att[:, 7168:8192].rearrange("p (a n) -> p a n", a=2)
        silu_buf = [sh_silu, xnT[:, :, 0:512]]
        h_buf = [sh_h, o_sb]
        w_gu = att[:, 0:4096].rearrange("p (w n) -> p w n", w=2 * KD)
        w_hi, w_lo = [[split[:, 1536 * f + 768 * n:1536 * f + 768 * (n + 1)] for f in range(FS // P)] for n in range(2)]
        x_hi, x_lo = [split[:, 12288 + 2048 * n:14336 + 2048 * n].rearrange("p (k n) -> p k n", k=KD) for n in range(2)]
        h_hi, h_lo = [[split[:, 16384 + 1536 * a + 512 * n:16896 + 1536 * a + 512 * n] for n in range(3)]
                      for a in range(2)]
        h_full = [att[:, 7168 + 512 * n:7680 + 512 * n] for n in range(3)]
        xnf = xn[:, :, :].rearrange("p c d -> p (c d)")
        e_xT = xnf[:, 0:512].rearrange("p (a k n) -> p a k n", a=2, k=KD)
        e_silu = xnf[:, 512:1536].rearrange("p (a n) -> p a n", a=2)
        e_h = xnf[:, 1536:2560].rearrange("p (a n) -> p a n", a=2)
        e_hT = xnf[:, 2560:3584].rearrange("p (a k n) -> p a k n", a=2, k=F // P)
        e_y = xnf[:, 3584:4096].rearrange("p (a n) -> p a n", a=2)
        gath = xnf.rearrange("p (a w n) -> p a w n", a=2, w=8)

        x_loaded = [sem(f"x_loaded{n}") for n in range(4)]
        proj_loaded = sem("proj_loaded")
        small_loaded = sem("small_loaded")
        mem_loaded = sem("mem_loaded")
        mem_zero = sem("mem_zero")
        router_zero = sem("router_zero")
        ident_zero = sem("ident_zero")
        ident_ready = sem("ident_ready")
        consts_ready = sem("consts_ready")
        slots_cleared = sem("slots_cleared")
        dve_step = sem("dve_step")
        act_step = sem("act_step")
        pool_step = sem("pool_step")
        var_ready = sem("var_ready")
        sd_ready = sem("sd_ready")
        xn_ready = sem("xn_ready")
        xT_in_psum = sem("xT_in_psum")
        xT_copied = sem("xT_copied")
        lT_in_psum = sem("lT_in_psum")
        lT_copied = sem("lT_copied")
        logits_in_psum = sem("logits_in_psum")
        logits_copied = sem("logits_copied")
        v_in_psum = sem("v_in_psum")
        v_copied = sem("v_copied")
        qk_in_psum = sem("qk_in_psum")
        qk_copied = sem("qk_copied")
        part_hi = sem("part_hi")
        residual = sem("residual")
        part_mid = sem("part_mid")
        part_lo = sem("part_lo")
        stacks_written = sem("stacks_written")
        q_min = sem("q_min")
        q_elu_parts = sem("q_elu_parts")
        sigma_ready = sem("sigma_ready")
        mem_in_psum = sem("mem_in_psum")
        mem_used = sem("mem_used")
        mem_added = sem("mem_added")
        experts_known = sem("experts_known")
        ranks_copied = sem("ranks_copied")
        mix_exp = sem("mix_exp")
        gap_ready = sem("gap_ready")
        gap_exp = sem("gap_exp")
        onehot_ready = sem("onehot_ready")
        ranks_in_psum = sem("ranks_in_psum")
        routed = sem("routed")
        scattered = sem("scattered")

        ones_rows = sem("ones_rows")
        stack_loaded = [sem(f"stack_loaded{n}") for n in range(4)]
        m_loaded = [sem(f"m_loaded{n}") for n in range(2)]
        a_ready = sem("a_ready")
        max_done = sem("max_done")
        maxT_in_psum = sem("maxT_in_psum")
        negm_ready = sem("negm_ready")
        m_hi = sem("m_hi")
        m_res = sem("m_res")
        m_mid = sem("m_mid")
        m_ready = sem("m_ready")
        scores_ready = sem("scores_ready")
        probs_ready = sem("probs_ready")
        v_head_ready = sem("v_head_ready")
        pv_done = sem("pv_done")
        o_copied = sem("o_copied")
        oT_in_psum = sem("oT_in_psum")
        oT_copied = sem("oT_copied")
        rden_ready = sem("rden_ready")
        o_ready = sem("o_ready")
        o_added = sem("o_added")

        w12_loaded = sem("w12_loaded")
        ex_loaded = [sem(f"ex_loaded{n}") for n in range(2)]
        exT_in_psum = sem("exT_in_psum")
        exT_ready = sem("exT_ready")
        up_done = sem("up_done")
        silu_done = sem("silu_done")
        h_ready = sem("h_ready")
        hT_in_psum = sem("hT_in_psum")
        hT_ready = sem("hT_ready")
        y_in_psum = sem("y_in_psum")
        y_ready = sem("y_ready")
        y_stored = [sem(f"y_stored{n}") for n in range(2)]
        shw_loaded = sem("shw_loaded")

        gathered = [sem(f"gathered{a}") for a in range(2)]
        s_up = sem("s_up")
        s_silu = sem("s_silu")
        s_h = sem("s_h")
        s_hused = sem("s_hused")
        s_down = sem("s_down")
        s_add = sem("s_add")
        s_mix = sem("s_mix")
        stored = sem("stored")
        x_hi_ready = sem("x_hi_ready")
        x_lo_ready = sem("x_lo_ready")
        w_hi_ready = sem("w_hi_ready")
        w_lo_ready = sem("w_lo_ready")
        h_hi_ready = sem("h_hi_ready")
        h_lo_ready = sem("h_lo_ready")

        block = ctx.enter_context(nc.Block())
        NF = FS // P

        RING = (4, 5, 7)
        TURNS, MAX_AT, OUT_AT = 18, 4, 13

        def turn_of(u):
            return u + (u >= MAX_AT) + (u >= OUT_AT - 1)

        UNITS = ((0, 2), (2, 5), (5, 8), (8, 12))

        def live(j):
            return not isinstance(j, int) or 0 <= j < TILES

        def over_tiles(eng, tile):
            for j in range(4):
                tile(j, j // 2, j % 2)
            with eng.Fori(2, TILES // 2 - 1) as pair:
                for a in range(2):
                    tile(pair * 2 + a, pair, a)
            for j in range(TILES // 2 * 2 - 2, TILES + 2):
                tile(j, j // 2, j % 2)

        FIRST = 2 * NF
        LAST = 2 * NF

        HIDDEN = {2: range(0, 4), 3: range(4, 9), 4: range(9, 14), 5: range(14, 19), 6: range(19, 25), 7: range(25, 32)}

        NLOOP = STEPS // 4
        PAIRS = STEPS // 2

        @block.sync
        def _(sp):
            for n in range(4):
                sp.dma_start(acc[:, 4 * n:4 * n + 4, :],
                             x_rows[512 * n:512 * (n + 1), :].rearrange("(c p) d -> p c d", p=P))\
                  .then_inc(x_loaded[n], 16)
            sp.dma_start(wkv_sb[:, :, 0:DKV], wkT.rearrange("(k p) n -> p k n", p=P)).then_inc(proj_loaded, 16)
            sp.dma_start(wq_sb, wqT.rearrange("(k p) n -> p k n", p=P)).then_inc(proj_loaded, 16)
            sp.dma_start(wkv_sb[:, :, DKV:2 * DKV], wvT.rearrange("(k p) n -> p k n", p=P)).then_inc(proj_loaded, 16)
            sp.wait_ge(router_zero, 1)
            sp.dma_start(router[:, :, 0:E], router_w.rearrange("(k p) n -> p k n", p=P)).then_inc(proj_loaded, 16)

            sp.dma_start(wg_sb, w_gate.rearrange("(k p) n -> p k n", p=P)).then_inc(shw_loaded, 16)
            sp.dma_start(wu_sb, w_up.rearrange("(k p) n -> p k n", p=P)).then_inc(shw_loaded, 16)
            sp.dma_start(wd_sb, w_down.rearrange("(k p) n -> p k n", p=P)).then_inc(shw_loaded, 16)
            sp.dma_start(mixw[:, 0:1], memory_weight.partition_broadcast(P)).then_inc(small_loaded, 16)
            sp.wait_ge(mem_zero, 1)
            for a in range(2):
                sp.dma_start(mem_w[DKV * a:DKV * (a + 1), MEMW * a:MEMW * a + DKV], memory).then_inc(mem_loaded, 16)
                sp.dma_start(mem_w[DKV * a:DKV * (a + 1), MEMW * a + DKV:MEMW * (a + 1)], memory_norm)\
                  .then_inc(mem_loaded, 16)
            sp.wait_ge(consts_ready, 1)
            sp.dma_start(slot_x.rearrange("(j p) d -> p j d", p=P),
                         zeros[:, :].unsqueeze(1).to_broadcast([P, TILES, D])).then_inc(slots_cleared, 16)
            for n in range(4):
                sp.dma_start(k_st[n][R:RM, :], ones[0:3, :]).then_inc(ones_rows, 16)
            for part, done in ((0, part_hi), (1, part_mid), (2, part_lo)):
                sp.wait_ge(done, 1)
                for c in range(NC):
                    if K_PART[c] == part:
                        sp.dma_start(k_stacks[:, DH * c:DH * (c + 1), :], kc[part][:, :]).then_inc(stacks_written, 16)
            for part, done in ((0, part_hi), (1, part_mid), (2, part_lo)):
                for m in range(KD):
                    sp.wait_ge(done, 2 + m)
                    for c in range(NC):
                        if Q_PART[c] == part:
                            sp.dma_start(q_stacks[2 * m:2 * m + 2, :, DH * c:DH * (c + 1), :], qc[part][:, m, :])\
                              .then_inc(stacks_written, 16)
            sp.wait_ge(stacks_written, 16 * NC * (1 + KD))

            def load_stack(b, h, n):
                sp.dma_start(q_st[n][0:R, :, :],
                             q_stacks[:, bass.ds(h, 1), :, bass.ds(b * SEQ, SEQ)].rearrange("g o r t -> r (o g) t"))\
                  .then_inc(stack_loaded[n], 16)
                sp.dma_start(k_st[n][0:R, :],
                             k_stacks[bass.ds(h, 1), :, bass.ds(b * SEQ, SEQ)].rearrange("o r t -> r (o t)"))\
                  .then_inc(stack_loaded[n], 16)

            def m_rows(i, s):
                sp.wait_ge(m_ready, i + 1)
                for c in range(3):
                    sp.dma_start(q_st[s % 4][R + c:R + c + 1, :, :].rearrange("o g s -> o (g s)"),
                                 m_parts[0:16, s % 2, c, :]).then_inc(m_loaded[s % 2], 16)

            sp.wait_ge(s_hused, NF)
            load_stack(0, 0, 0)
            load_stack(0, 1, 1)
            sp.wait_ge(s_hused, 2 * NF)
            load_stack(0, 2, 2)
            def steps(b, h0, last):
                for s in range(4):
                    i = b * H + (h0 + s)
                    m_rows(i, s)
                    if last and s > 0:
                        continue
                    wait(sp, scores_ready, i * 16)
                    if h0 == 4 and s > 0:
                        load_stack(b + 1, s - 1, (s + 3) % 4)
                    else:
                        load_stack(b, h0 + s + 3, (s + 3) % 4)
            steps(0, 0, False)
            steps(0, 4, False)
            with sp.Fori(1, BATCH - 1) as b:
                steps(b, 0, False)
                steps(b, 4, False)
            steps(BATCH - 1, 0, False)

            def load_x(j, a):
                wait(sp, exT_in_psum, j - 1)
                sp.dma_start(e_x[:, a, :], slot_x[bass.ds(j * P, P), :]).then_inc(ex_loaded[a], 16)

            sp.wait_ge(scattered, 16 * TOPK * NT)
            load_x(0, 0)
            load_x(1, 1)
            steps(BATCH - 1, 4, True)

            def store_y(j, a):
                sp.wait_ge(y_ready, j + 1)
                sp.dma_start(slot_y[bass.ds(j * P, P), :], e_y[:, a, :]).then_inc(y_stored[a], 16)

            def tile(j, pair, a):
                if live(j + 2):
                    load_x(j + 2, a)
                if live(j - 2):
                    store_y(j - 2, a)

            over_tiles(sp, tile)

            for n in range(3):
                sp.wait_ge(s_mix, (n + 1) * 8)
                sp.wait_ge(s_add, max(n + 1, 2) * 4)
                sp.dma_start(out_rows[n * 512:(n + 1) * 512, :].rearrange("(c p) d -> p c d", p=P),
                             acc[:, n * 4:(n + 1) * 4, :]).then_inc(stored, 16)
            for c in range(NT - 4, NT):
                sp.wait_ge(s_mix, NT * TOPK)
                sp.wait_ge(s_add, c + 1)
                sp.dma_start(out_rows[c * P:(c + 1) * P, :], acc[:, c, :]).then_inc(stored, 16)
            sp.wait_ge(stored, 16 * (3 + 4))

        @block.gpsimd
        def _(pool):
            count = [0]

            def link(ins):
                count[0] += 1
                ins.then_inc(pool_step, 1)
                pool.wait_ge(pool_step, count[0])

            pool.memset(ident[:, :], 0.0).then_inc(ident_zero, 1)
            pool.wait_ge(ident_zero, 1)
            pool.affine_select(out=ident[:, :], in_=ident[:, :], compare_op=ALU.not_equal, fill=1.0,
                               base=0, pattern=[[-1, P]], channel_multiplier=1).then_inc(ident_ready, 1)
            pool.memset(router[:, :, :], 0.0).then_inc(router_zero, 1)
            pool.memset(mem_w[:, :], 0.0).then_inc(mem_zero, 1)
            pool.memset(zeros[:, :], 0.0)
            pool.memset(v_head[:, :, :, :], 0.0)
            link(pool.memset(ones[:, :], 1.0))
            for a in range(2):
                pool.memset(v_head[:, a, :, (DH + 1) * a + DH:(DH + 1) * (a + 1)], 1.0)
            pool.iota(iota_e[:, :], pattern=[[1, E]], base=0, channel_multiplier=0,
                      allow_small_or_imprecise_dtypes=True)
            pool.iota(iota_t[:, :], pattern=[[1, TILES]], base=0, channel_multiplier=0,
                      allow_small_or_imprecise_dtypes=True)
            pool.iota(full_at[:, :], pattern=[[P, NT]], base=0, channel_multiplier=0,
                      allow_small_or_imprecise_dtypes=True)
            pool.affine_select(out=before[:, :], in_=ones[:, 0:P], compare_op=ALU.is_gt, fill=0.0,
                               base=0, pattern=[[1, P]], channel_multiplier=-1).then_inc(consts_ready, 1)

            def scatter(first, count):
                for n in range(first, first + count):
                    pool.indirect_dma_start(
                        out=slot_x, out_offset=bass.IndirectOffsetOnAxis(ap=slot[:, n:n + 1], axis=0),
                        in_=xn[:, n % NT, :], in_offset=None).then_inc(scattered, 16)

            pool.wait_ge(v_copied, 2)

            def stage_v(i, b, h, s):
                wait(pool, pv_done, ST * (i - 1))
                first = (DH + 1) * (s % 2)
                pool.tensor_copy(v_head[:, s % 2, :, first:first + DH],
                                 v_all[:, bass.ds(b * ST, ST), bass.ds(h * DH, DH)]).then_inc(v_head_ready, 1)

            def split_m(i, s, pairs):
                a = s % 2
                pool.wait_ge(negm_ready, i + 1)
                wait(pool, m_loaded[a], pairs * 48)
                pool.tensor_tensor(m_parts[:, a, 0, :], negm[:, a, :], zeros[0:16, 0:P], ALU.subtract).then_inc(m_hi, 1)
                pool.wait_ge(m_hi, i + 1)
                pool.tensor_tensor(negr[:, a, :], negm[:, a, :], m_parts[:, a, 0, :], ALU.subtract).then_inc(m_res, 1)
                pool.wait_ge(m_res, i + 1)
                pool.tensor_tensor(m_parts[:, a, 1, :], negr[:, a, :], zeros[0:16, 0:P], ALU.subtract).then_inc(m_mid, 1)
                pool.wait_ge(m_mid, i + 1)
                pool.tensor_tensor(m_parts[:, a, 2, :], negr[:, a, :], m_parts[:, a, 1, :], ALU.subtract)\
                    .then_inc(m_ready, 1)

            def add_o(pair, a, b, h):
                pool.wait_ge(o_ready, pair + 1)
                place = acc[:, bass.ds(b * ST, ST), :].rearrange("p t (g c) -> p t g c", g=G)[
                    :, :, :, bass.ds(h * DH, 2 * DH)]
                pool.tensor_tensor(place, place,
                                   otmp[:, a, :, :].rearrange("p (t g two) d -> p t g (two d)", t=ST, g=G),
                                   ALU.add).then_inc(o_added, 1)

            stage_v(0, 0, 0, 0)
            split_m(0, 0, 0)

            pool.wait_ge(s_add, 2 * 4)
            for n in range(NT // 2):
                pool.wait_ge(mem_used, n + 1)
                place = acc[:, 2 * n:2 * n + 2, :]
                pool.tensor_tensor(place, place, mtmp[:, 2 * (n % 4):2 * (n % 4) + 2, :], ALU.add)\
                    .then_inc(mem_added, 1)
            pool.wait_ge(mem_added, NT // 2)
            pool.wait_ge(routed, 1)
            pool.wait_ge(slots_cleared, 16)

            SCATTERS = {1: (0, 5), 2: (5, 5), 3: (10, 5), 4: (15, 5), 5: (20, 4), 6: (24, 4), 7: (28, 4)}

            def steps(blk, b, h0, first=False):
                for s in range(4):
                    i = blk * 4 + s
                    if not (first and s == 0):
                        stage_v(i, b, h0 + s, s)
                        split_m(i, s, blk * 2 + s // 2)
                    if isinstance(i, int) and 1 <= i < 8:
                        scatter(*SCATTERS[i])
                    if s == 1 and not first:
                        add_o(blk * 2 - 1, 1, b if h0 == 4 else b - 1, (h0 - 2) % H)
                    if s == 3:
                        add_o(blk * 2, 0, b, h0)

            steps(0, 0, 0, first=True)
            steps(1, 0, 4)
            with pool.Fori(1, BATCH) as b:
                steps(b * 2, b, 0)
                steps(b * 2 + 1, b, 4)
            add_o(PAIRS - 1, 1, BATCH - 1, H - 2)

            for a in range(2):
                pool.wait_ge(y_stored[a], 16 * ((TILES + 1 - a) // 2))
            for n in range(NT // 4):
                wait(pool, s_mix, 8 * (n - 1))
                for c in range(4):
                    for k in range(TOPK):
                        w = k * NT + 4 * n + c
                        pool.indirect_dma_start(
                            out=gath[:, n % 2, 2 * c + k, :], out_offset=None, in_=slot_y,
                            in_offset=bass.IndirectOffsetOnAxis(ap=slot[:, w:w + 1], axis=0)).then_inc(gathered[n % 2], 16)

        @block.scalar
        def _(act):
            def sqrt_var(n):
                act.wait_ge(var_ready, n + 1)
                act.activation(sd[:, 4 * n:4 * n + 4], meanvar[:, 4 * n:4 * n + 4, 1], ACT.Sqrt).then_inc(sd_ready, 1)

            def copy_xT(n):
                act.wait_ge(xT_in_psum, n + 1)
                act.activation(xnT[:, n % 2, 512 * (n // 2):512 * (n // 2 + 1)], ps[:, n % 4, :], ACT.Copy)\
                   .then_inc(xT_copied, 1)

            def copy_qk(u):
                n, part = divmod(u, 3)
                act.wait_ge(qk_in_psum, u + 1)
                if part == 0:
                    ins = act.activation(kv[:, 512 * n:512 * (n + 1)], ps[:, 4 + u % 4, :], ACT.Copy)
                else:
                    ins = act.activation(qf[:, part - 1, 512 * n:512 * (n + 1)], ps[:, 4 + u % 4, :], ACT.Copy)
                ins.then_inc(qk_copied, 1)

            for n in range(4):
                sqrt_var(n)
                copy_xT(2 * n)
                copy_xT(2 * n + 1)
                if n > 0:
                    for u in range(*UNITS[n - 1]):
                        copy_qk(u)
            for u in range(*UNITS[3]):
                copy_qk(u)
            act.wait_ge(lT_in_psum, 1)
            act.activation(o_sb[:, 0, :], ps[:, 1, :], ACT.Copy).then_inc(lT_copied, 1)
            for half, bank in enumerate((0, 3)):
                act.wait_ge(v_in_psum, half + 1)
                act.activation(v_all[:, 8 * half:8 * half + 8, :].rearrange("p c n -> p (c n)"), ps[:, bank, :],
                               ACT.Copy).then_inc(v_copied, 1)
            act.wait_ge(qk_copied, 12)
            act.activation(kc[0], kf, ACT.Copy).then_inc(part_hi, 1)
            act.wait_ge(small_loaded, 16)
            act.activation(mixw[:, 1:2], mixw[:, 0:1], ACT.Exp, scale=-1.0).then_inc(mix_exp, 1)
            act.wait_ge(gap_ready, 1)
            act.activation(score[:, 1, :], score[:, 1, :], ACT.Exp).then_inc(gap_exp, 1)

            def silu_shared(n, f):
                act.wait_ge(s_up, n * (2 * NF) + (2 * f + 1))
                wait(act, s_h, n * NF + max(f - 1, 0))
                act.activation(silu_buf[n][:, f % 2, :], ps[:, f % 2 * (1 - n), :], ACT.Silu).then_inc(s_silu, 1)

            def q_hi(m):
                act.activation(qc[0][:, m, :], qf[:, m, :], ACT.Copy).then_inc(part_hi, 1)

            def k_mid():
                act.wait_ge(residual, 1)
                act.activation(kc[1], kr, ACT.Copy).then_inc(part_mid, 1)

            def q_mid(m):
                act.wait_ge(residual, 2 + m)
                act.activation(qc[1][:, m, :], qr[:, m, :], ACT.Copy).then_inc(part_mid, 1)

            def q_tanh():
                act.wait_ge(q_elu_parts, 1)
                act.activation(qr, qr, ACT.Tanh, scale=0.5).then_inc(q_elu_parts, 1)

            def q_exp():
                act.wait_ge(q_min, 1)
                act.activation(qe, qr, ACT.Exp).then_inc(q_elu_parts, 1)

            between = {(0, 0): lambda: q_hi(0), (0, 1): lambda: (k_mid(), q_hi(1)),
                       (0, 3): lambda: q_mid(0), (0, 4): lambda: q_mid(1),
                       (0, 7): q_exp, (1, 0): q_tanh}
            for n in range(2):
                for f in range(NF):
                    silu_shared(n, f)
                    if (n, f) in between:
                        between[n, f]()

            def negate_max(i, s):
                act.wait_ge(maxT_in_psum, i + 1)
                wait(act, m_ready, i - 1)
                act.activation(negm[:, s % 2, :], ps[0:16, RING[MAX_AT % 3], 0:P], ACT.Copy, scale=-1.0)\
                   .then_inc(negm_ready, 1)

            def evacuate_o(pair, a):
                act.wait_ge(pv_done, 2 * ST * (pair + 1))
                wait(act, oT_in_psum, pair - 1)
                act.activation(o_sb[:, a, :], ps[:, 6, :], ACT.Copy).then_inc(o_copied, 1)

            def copy_oT(pair, a):
                act.wait_ge(oT_in_psum, pair + 1)
                wait(act, o_ready, pair - 1)
                act.activation(oT_sb[:, a, :, :].rearrange("p (w two) n -> p w (two n)", two=2),
                               ps[:, RING[OUT_AT % 3], :].rearrange("p (w n) -> p w n", n=32)[:, :, 0:2 * (DH + 1)],
                               ACT.Copy).then_inc(oT_copied, 1)

            def copy_ex(j, a):
                act.wait_ge(exT_in_psum, j + 1)
                wait(act, up_done, (j - 1) * 2)
                act.activation(e_xT[:, a, :, :], ps[:, 2, 0:D].rearrange("p (k n) -> p k n", k=KD), ACT.Copy)\
                   .then_inc(exT_ready, 1)

            def exps(blk, s, first=False, last=False):
                i = blk * 4 + s
                for u in range(16):
                    t, g = divmod(u, G)
                    if u == 4 and not last:
                        negate_max(i + 1, s + 1)
                    if u == 7 and last:
                        act.wait_ge(scattered, 16 * TOPK * NT)
                        copy_ex(0, 0)
                    if s % 2 == 0 and not first:
                        if u == 5:
                            evacuate_o(blk * 2 + (s // 2 - 1), (s // 2 + 1) % 2)
                        if u == 12:
                            copy_oT(blk * 2 + (s // 2 - 1), (s // 2 + 1) % 2)
                    act.wait_ge(scores_ready, i * 16 + (u + 1))
                    if g == 0:
                        wait(act, pv_done, i * ST + (t - 1))
                    act.activation(probs[:, t % 2, g, :], ps[:, RING[turn_of(u) % 3], :], ACT.Exp, scale=SCALE)\
                       .then_inc(probs_ready, 1)

            def load_expert(n):
                act.dma_start(w1_sb[:, n, :, :], w1[n].rearrange("(k p) n -> p k n", p=P)).then_inc(w12_loaded, 16)
                act.dma_start(w2_sb[:, n, :, :], w2[n].rearrange("(k p) n -> p k n", p=P)).then_inc(w12_loaded, 16)

            LATE = {-4: (4, 5), -3: (6,), -2: (7,), -1: ()}
            negate_max(0, 0)
            for i in range(4):
                exps(0, i, first=i == 0)
                if i == 0:
                    act.wait_ge(mem_added, NT // 2)
                    act.wait_ge(stacks_written, 16 * NC * (1 + KD))
                load_expert(i)
            with act.Fori(1, NLOOP - 1) as blk:
                for s in range(4):
                    exps(blk, s)
            for i in range(STEPS - 4, STEPS):
                for n in LATE[i - STEPS]:
                    load_expert(n)
                exps(NLOOP - 1, i % 4, last=i == STEPS - 1)
            copy_ex(1, 1)
            evacuate_o(PAIRS - 1, 1)
            copy_oT(PAIRS - 1, 1)

            def load_shared():
                act.wait_ge(pv_done, ST * STEPS)
                act.dma_start(wg_sb, w_gate.rearrange("(k p) n -> p k n", p=P)).then_inc(shw_loaded, 16)
                act.dma_start(wu_sb, w_up.rearrange("(k p) n -> p k n", p=P)).then_inc(shw_loaded, 16)
                act.dma_start(wd_sb, w_down.rearrange("(k p) n -> p k n", p=P)).then_inc(shw_loaded, 16)

            def split_x(n):
                act.activation(x_hi[:, :, 512 * n:512 * (n + 1)], xnT[:, :, 512 * (n + 2):512 * (n + 3)], ACT.Copy)\
                   .then_inc(x_hi_ready, 1)

            def split_w(f):
                act.activation(w_hi[f][:, 0:512].rearrange("p (w n) -> p w n", w=2 * KD),
                               w_gu[:, :, P * f:P * (f + 1)], ACT.Copy)
                act.activation(w_hi[f][:, 512:768], wd_sb[:, f, :], ACT.Copy).then_inc(w_hi_ready, 1)

            def silu_g(j, a):
                act.wait_ge(up_done, j * 2 + 1)
                wait(act, h_ready, j - 1)
                act.activation(e_silu[:, a, :], ps[:, 4 * a, :], ACT.Silu).then_inc(silu_done, 1)

            def copy_y(j, pair, a):
                act.wait_ge(y_in_psum, j + 1)
                wait(act, y_stored[a], pair * 16)
                act.activation(e_y[:, a, :], ps[:, 6 + a, 0:D], ACT.Copy).then_inc(y_ready, 1)

            def tile(j, pair, a):
                if live(j):
                    silu_g(j, a)
                if live(j + 1) and not (isinstance(j, int) and j == 0):
                    copy_ex(j + 1, 1 - a)
                if isinstance(j, int) and j == TILES + 1:
                    act.wait_ge(y_in_psum, TILES)
                    act.wait_ge(shw_loaded, 96)
                    split_x(0)
                    split_w(0)
                if live(j - 2):
                    copy_y(j - 2, pair - 1, a)
                if isinstance(j, int) and j == 3:
                    load_shared()
            over_tiles(act, tile)

            split_w(1)
            for m in range(LAST):
                act.wait_ge(s_up, 2 * (FIRST + m) + 1)
                act.wait_ge(s_h, FIRST + max(m - 1, 0))
                act.activation(sh_silu[:, m % 2, :], ps[:, m % 2, :], ACT.Silu).then_inc(s_silu, 1)
                if m == 2:
                    split_x(1)
                if m + 2 < NF:
                    split_w(m + 2)
                act.wait_ge(s_h, FIRST + m + 1)
                wait(act, s_hused, FIRST + m - 2 if m > 2 else 0)
                act.activation(h_hi[m % 3], h_full[m % 3], ACT.Copy).then_inc(h_hi_ready, 1)

        @block.vector
        def _(dve):
            count = [0]

            def link(ins):
                count[0] += 1
                ins.then_inc(dve_step, 1)
                dve.wait_ge(dve_step, count[0])

            for n in range(4):
                tiles = range(4 * n, 4 * n + 4)
                part = slice(4 * n, 4 * n + 4)
                dve.wait_ge(x_loaded[n], 16)
                for c in tiles:
                    last = dve.bn_stats(stats[:, c, :], acc[:, c, :])
                link(last)
                for c in tiles:
                    last = dve.bn_aggr(meanvar[:, c, :], stats[:, c, :])
                link(last)
                dve.tensor_scalar_add(meanvar[:, part, 1], meanvar[:, part, 1], EPS).then_inc(var_ready, 1)
                dve.wait_ge(sd_ready, n + 1)
                link(dve.reciprocal(rstd[:, part], sd[:, part]))
                link(dve.tensor_tensor(sd[:, part], rstd[:, part], rstd[:, part], ALU.mult))
                link(dve.tensor_tensor(sd[:, part], sd[:, part], meanvar[:, part, 1], ALU.mult))
                link(dve.tensor_scalar(sd[:, part], sd[:, part], -0.5, 1.5, ALU.mult, ALU.add))
                link(dve.tensor_tensor(rstd[:, part], rstd[:, part], sd[:, part], ALU.mult))
                for c in tiles:
                    dve.tensor_scalar(xn[:, c, :], acc[:, c, :], meanvar[:, c, 0:1], rstd[:, c:c + 1],
                                      ALU.subtract, ALU.mult).then_inc(xn_ready, 1)

            dve.wait_ge(logits_in_psum, 1)
            dve.tensor_copy(logits[:, :, :].rearrange("p (g t) e -> p g t e", g=4),
                            ps[:, 2, :].rearrange("p (t g e) -> p g t e", t=4, g=4)[:, :, :, 0:E])\
               .then_inc(logits_copied, 1)
            dve.wait_ge(logits_copied, 1)
            for c in range(NT):
                last = dve.max(top[:, c, :], logits[:, c, :])
            link(last)
            for c in range(NT):
                last = dve.max_index(topi[:, c, :], top[:, c, :], logits[:, c, :])
            link(last)
            dve.tensor_tensor(score[:, 1, :], top[:, :, 1], top[:, :, 0], ALU.subtract).then_inc(gap_ready, 1)
            link(dve.tensor_copy(choice[:, :, :], topi[:, :, 0:TOPK].rearrange("p c k -> p k c")))
            dve.wait_ge(consts_ready, 1)
            W = TOPK * NT
            dve.tensor_tensor(onehot[:, :, :],
                              choice[:, :, :].rearrange("p k c -> p (k c)").unsqueeze(2).to_broadcast([P, W, E]),
                              iota_e[:, :].unsqueeze(1).to_broadcast([P, W, E]), ALU.is_equal)\
               .then_inc(onehot_ready, 1)

            def res(n, f, r, c):
                dve.wait_ge(part_hi, n)
                dve.tensor_tensor(r, f, c, ALU.subtract).then_inc(residual, 1)

            def low(n, r, c, out_part):
                dve.wait_ge(part_mid, n)
                dve.wait_ge(residual, n)
                dve.tensor_tensor(out_part, r, c, ALU.subtract).then_inc(part_lo, 1)

            def elu_min():
                dve.wait_ge(part_lo, 3)
                dve.tensor_scalar_min(qr, qf, 0.0).then_inc(q_min, 1)

            def elu_mult(m):
                dve.wait_ge(q_elu_parts, 2)
                link(dve.scalar_tensor_tensor(qr[:, m, :], qe[:, m, :], 1.0, qr[:, m, :], ALU.add, ALU.mult))

            def elu_add(m):
                dve.scalar_tensor_tensor(qf[:, m, :], qf[:, m, :], 0.0, qr[:, m, :], ALU.max, ALU.add)\
                   .then_inc(sigma_ready, 1)

            def copy_ranks():
                dve.wait_ge(ranks_in_psum, 1)
                dve.tensor_copy(rank[:, :, :].rearrange("p w e -> p (w e)"), ps[:, 3, 0:W * E])
                ins = dve.tensor_copy(total[:, :, :].rearrange("p w e -> p (w e)"), ps[:, 3, W * E:2 * W * E])
                ins.then_inc(ranks_copied, 1)
                dve.wait_ge(ranks_copied, 1)

            chunk_sum, chunk_tmp = run_a, run_b
            expert_sum, expert_tmp = cum_a, cum_b

            def sum_chunks():
                src, dst, other = total, run_a, run_b
                step = 1
                while step < W:
                    dve.tensor_copy(dst[:, 0:step, :], src[:, 0:step, :])
                    link(dve.tensor_tensor(dst[:, step:W, :], src[:, step:W, :], src[:, 0:W - step, :], ALU.add))
                    src, dst, other = dst, other, dst
                    step *= 2
                assert src is chunk_sum

            def count_tiles():
                link(dve.tensor_tensor(gt, chunk_sum[:, W - 1, :].unsqueeze(2).to_broadcast([P, E, NT]),
                                       full_at[:, :].unsqueeze(1).to_broadcast([P, E, NT]), ALU.is_gt))
                link(dve.tensor_reduce(tiles_e[:, :], gt, X_AXIS, ALU.add))
                csrc, cdst, cother = tiles_e, cum_a, cum_b
                step = 1
                while step < E:
                    dve.tensor_copy(cdst[:, 0:step], csrc[:, 0:step])
                    link(dve.tensor_tensor(cdst[:, step:E], csrc[:, step:E], csrc[:, 0:E - step], ALU.add))
                    csrc, cdst, cother = cdst, cother, cdst
                    step *= 2
                assert csrc is expert_sum
                link(dve.tensor_tensor(le, expert_sum[:, :].unsqueeze(1).to_broadcast([P, TILES, E]),
                                       iota_t[:, :].unsqueeze(2).to_broadcast([P, TILES, E]), ALU.is_le))
                link(dve.tensor_reduce(expert_f[:, :], le, X_AXIS, ALU.add))
                dve.tensor_scalar_min(expert[:, :], expert_f[:, :], float(E - 1)).then_inc(experts_known, 1)

            def find_slots():
                link(dve.tensor_tensor(expert_tmp[:, :], expert_sum[:, :], tiles_e[:, :], ALU.subtract))
                link(dve.tensor_tensor(chunk_tmp, chunk_sum, total, ALU.subtract))
                link(dve.tensor_tensor(rank, rank, chunk_tmp, ALU.add))
                link(dve.scalar_tensor_tensor(chunk_tmp, expert_tmp[:, :].unsqueeze(1).to_broadcast([P, W, E]),
                                              float(P), rank, ALU.mult, ALU.add))
                link(dve.tensor_tensor(rank, chunk_tmp, onehot[:, :, :], ALU.mult))
                link(dve.tensor_reduce(slot_f[:, :], rank, X_AXIS, ALU.add))
                dve.tensor_copy(slot[:, :], slot_f[:, :]).then_inc(routed, 1)

            def weights_of_terms():
                dve.wait_ge(gap_exp, 1)
                link(dve.tensor_scalar_add(score[:, 0, :], score[:, 1, :], 1.0))
                link(dve.reciprocal(score[:, 0, :], score[:, 0, :]))
                dve.tensor_tensor(score[:, 1, :], score[:, 1, :], score[:, 0, :], ALU.mult)
                dve.wait_ge(mix_exp, 1)
                link(dve.tensor_scalar_add(mixw[:, 2:3], mixw[:, 1:2], 1.0))
                link(dve.reciprocal(mixw[:, 2:3], mixw[:, 2:3]))
                link(dve.tensor_scalar(mixw[:, 3:4], mixw[:, 2:3], -1.0, 1.0, ALU.mult, ALU.add))

            def shared_h(n, f):
                dve.wait_ge(s_silu, n * NF + (f + 1))
                dve.wait_ge(s_up, n * (2 * NF) + (2 * f + 2))
                wait(dve, s_hused, n * NF + max(f - 1, 0))
                dve.tensor_tensor(h_buf[n][:, f % 2, :], silu_buf[n][:, f % 2, :],
                                  ps[:, 1 if n == 1 else 2 + f % 2, :], ALU.mult).then_inc(s_h, 1)

            def row_of(c):
                return acc[:, bass.ds(c, 1), :].rearrange("p o d -> p (o d)")

            def add_shared(n):
                dve.wait_ge(s_hused, n * NF + NF)
                for c in range(4):
                    row = row_of(n * 4 + c)
                    dve.tensor_tensor(row, row, ps[:, 4 + c, 0:D], ALU.add).then_inc(s_add, 1)

            def maxima(i, s, u, bank=None):
                dve.wait_ge(a_ready, i * 16 + (u + 1))
                if u == 0:
                    wait(dve, maxT_in_psum, i - 1)
                dve.reduce_max(smax[:, s % 2, u:u + 1], ps[:, u % 4 if bank is None else bank, :], X_AXIS).then_inc(max_done, 1)

            res(1, kf, kr, kc[0])
            between = {
                (0, 1): lambda: res(2, qf[:, 0, :], qr[:, 0, :], qc[0][:, 0, :]),
                (0, 2): lambda: (low(1, kr, kc[1], kc[2]), res(3, qf[:, 1, :], qr[:, 1, :], qc[0][:, 1, :])),
                (0, 4): lambda: low(2, qr[:, 0, :], qc[1][:, 0, :], qc[2][:, 0, :]),
                (0, 5): lambda: (low(3, qr[:, 1, :], qc[1][:, 1, :], qc[2][:, 1, :]), elu_min()),
                (0, 6): weights_of_terms,
                (1, 0): sum_chunks,
                (1, 1): count_tiles,
                (1, 2): find_slots,
                (1, 3): lambda: elu_mult(0),
                (1, 4): lambda: elu_add(0),
                (1, 5): lambda: elu_mult(1),
                (1, 6): lambda: elu_add(1),
            }
            for n in range(2):
                for f in range(NF):
                    tiles = HIDDEN.get(f, ()) if n == 1 else ()
                    for v in tiles[:4]:
                        maxima(v // 16, v // 16, v % 16, 2 + v % 2)
                    shared_h(n, f)
                    if (n, f) == (1, 0):
                        add_shared(0)
                        copy_ranks()
                    for v in tiles[4:]:
                        maxima(v // 16, v // 16, v % 16, 2 + v % 2)
                    if (n, f) in between:
                        between[n, f]()
            add_shared(1)
            dve.wait_ge(s_add, 2 * 4)
            for n in range(NT // 2):
                dve.wait_ge(mem_in_psum, n + 1)
                read = ps[:, 2 * (n % 2):2 * (n % 2) + 2, 0:G * MEMW].rearrange("p a (g n) -> p a g n", g=G)
                link(dve.reciprocal(mden[:, n % 2, :, :], read[:, :, :, DKV]))
                wait(dve, mem_added, n - 3)
                for a in range(2):
                    last = dve.scalar_tensor_tensor(
                        mtmp[:, 2 * (n % 4) + a, :].rearrange("p (g n) -> p g n", g=G), read[:, a, :, 0:DKV],
                        mixw[:, 2:3], mden[:, n % 2, a, :].unsqueeze(2).to_broadcast([P, G, DKV]),
                        ALU.mult, ALU.mult)
                last.then_inc(mem_used, 1)

            def finish_o(pair, a):
                dve.wait_ge(oT_copied, pair + 1)
                wait(dve, o_added, pair - 1)
                o = oT_sb[:, a, :, :]
                dve.reciprocal(rden[:, a, :], o[:, :, DH]).then_inc(rden_ready, 1)
                dve.wait_ge(rden_ready, pair + 1)
                dve.scalar_tensor_tensor(otmp[:, a, :, :], o[:, :, 0:DH], mixw[:, 3:4],
                                         rden[:, a, :].unsqueeze(2).to_broadcast([P, 32, DH]), ALU.mult, ALU.mult)\
                   .then_inc(o_ready, 1)

            def step(blk, s, first=False, ahead=True):
                i = blk * 4 + s
                for u in range(16):
                    if u == 15 and s % 2 == 0 and not first:
                        finish_o(blk * 2 + (s // 2 - 1), (s // 2 + 1) % 2)
                    if ahead:
                        maxima(i + 2, s, u)

            for i in range(4):
                step(0, i, first=i == 0)
            with dve.Fori(1, NLOOP - 1) as blk:
                for s in range(4):
                    step(blk, s)
            for i in range(STEPS - 4, STEPS):
                step(NLOOP - 1, i % 4, ahead=i + 2 < STEPS)
            finish_o(PAIRS - 1, 1)

            def copy_hT(j, a):
                dve.wait_ge(hT_in_psum, j + 1)
                wait(dve, y_in_psum, j - 1)
                dve.tensor_copy(e_hT[:, a, :, :].rearrange("p k n -> p (k n)"), ps[:, 3, :]).then_inc(hT_ready, 1)

            def make_h(j, a):
                dve.wait_ge(silu_done, j + 1)
                dve.wait_ge(up_done, j * 2 + 2)
                wait(dve, hT_in_psum, j - 1)
                dve.tensor_tensor(e_h[:, a, :], e_silu[:, a, :], ps[:, 4 * a + 1, :], ALU.mult).then_inc(h_ready, 1)

            def tile(j, pair, a):
                if live(j - 1):
                    copy_hT(j - 1, 1 - a)
                if live(j):
                    make_h(j, a)

            def low_x(n):
                dve.wait_ge(x_hi_ready, n + 1)
                dve.tensor_tensor(x_lo[:, :, 512 * n:512 * (n + 1)], xnT[:, :, 512 * (n + 2):512 * (n + 3)],
                                  x_hi[:, :, 512 * n:512 * (n + 1)], ALU.subtract).then_inc(x_lo_ready, 1)

            def low_w(f):
                dve.wait_ge(w_hi_ready, f + 1)
                dve.tensor_tensor(w_lo[f][:, 0:512].rearrange("p (w n) -> p w n", w=2 * KD),
                                  w_gu[:, :, P * f:P * (f + 1)],
                                  w_hi[f][:, 0:512].rearrange("p (w n) -> p w n", w=2 * KD), ALU.subtract)
                dve.tensor_tensor(w_lo[f][:, 512:768], wd_sb[:, f, :], w_hi[f][:, 512:768], ALU.subtract)\
                   .then_inc(w_lo_ready, 1)

            over_tiles(dve, tile)

            dve.wait_ge(o_added, PAIRS)

            def mix(batch, k):
                half = batch % 2
                dve.wait_ge(gathered[half], (batch // 2 + 1) * (16 * 8))
                dve.wait_ge(s_add, 4 * max(batch, 2))
                for c in range(4):
                    row = acc[:, batch * 4 + c, :]
                    if k == 1:
                        dve.wait_ge(s_mix, batch * 8 + (c + 1))
                    dve.scalar_tensor_tensor(row, gath[:, half, 2 * c + k, :],
                                             score[:, k, batch * 4 + c:batch * 4 + c + 1], row,
                                             ALU.mult, ALU.add).then_inc(s_mix, 1)

            MIXES = {3: (0, 0), 4: (0, 1), 5: (1, 0), 6: (1, 1), 10: (2, 0), 11: (2, 1), 12: (3, 0), 13: (3, 1)}
            low_x(0)
            low_w(0)
            low_w(1)
            for m in range(LAST):
                dve.wait_ge(s_silu, FIRST + m + 1)
                dve.wait_ge(s_up, 2 * (FIRST + m) + 2)
                wait(dve, s_hused, FIRST + m - 2 if m > 2 else 0)
                dve.tensor_tensor(h_full[m % 3], sh_silu[:, m % 2, :], ps[:, 2 + m % 2, :], ALU.mult).then_inc(s_h, 1)
                if m == 2:
                    low_x(1)
                dve.wait_ge(h_hi_ready, m + 1)
                dve.tensor_tensor(h_lo[m % 3], h_full[m % 3], h_hi[m % 3], ALU.subtract).then_inc(h_lo_ready, 1)
                if m + 2 < NF:
                    low_w(m + 2)
                if m == NF + 1:
                    add_shared(2)
                if m in MIXES:
                    mix(*MIXES[m])
            dve.wait_ge(s_mix, NT * TOPK)
            add_shared(3)

        @block.tensor
        def _(pe):
            pe.wait_ge(ident_ready, 1)

            def transpose_xn(g):
                for c in range(4):
                    pe.wait_ge(xn_ready, 4 * g + c + 1)
                    for m in range(KD):
                        n = 2 * g + m
                        if n >= 4 and c == 0:
                            pe.wait_ge(xT_copied, n - 3)
                        ins = pe.transpose(ps[:, n % 4, P * c:P * (c + 1)], xn[:, 4 * g + c, P * m:P * (m + 1)],
                                           ident[:, :])
                        if c == 3:
                            ins.then_inc(xT_in_psum, 1)

            def project_qk(u):
                n, part = divmod(u, 3)
                pe.wait_ge(xT_copied, 2 * n + 2)
                wait(pe, qk_copied, u - 3)
                for k in range(KD):
                    tokens = xnT[:, k, 512 * n:512 * (n + 1)]
                    if part == 0:
                        last = pe.matmul(ps[:, 4 + u % 4, :], wkv_sb[:, k, :], tokens,
                                         start=k == 0, stop=k == KD - 1)
                    else:
                        last = pe.matmul(ps[:, 4 + u % 4, :], wq_sb[:, k, P * (part - 1):P * part], tokens,
                                         start=k == 0, stop=k == KD - 1)
                last.then_inc(qk_in_psum, 1)

            for n in range(4):
                transpose_xn(n)
                if n == 0:
                    pe.wait_ge(proj_loaded, 64)
                for u in range(*UNITS[n]):
                    project_qk(u)
            for k in range(KD):
                for g in range(4):
                    last = pe.matmul(ps[32 * g:32 * (g + 1), 1, :], router[:, k, :], xnT[:, k, 512 * g:512 * (g + 1)],
                                     start=k == 0, stop=k == KD - 1)
            last.then_inc(lT_in_psum, 1)
            pe.wait_ge(qk_copied, 10)
            for c in range(NT):
                last = pe.transpose(ps[:, 3 * (c // 8), DKV * (c % 8):DKV * (c % 8 + 1)],
                                    kv[DKV:2 * DKV, P * c:P * (c + 1)], ident[DKV:2 * DKV, DKV:2 * DKV])
                if c % 8 == 7:
                    last.then_inc(v_in_psum, 1)
            pe.wait_ge(lT_copied, 1)
            for t in range(4):
                last = pe.transpose(ps[:, 2, P * t:P * (t + 1)], o_sb[:, 0, P * t:P * (t + 1)], ident[:, :])
            last.then_inc(logits_in_psum, 1)

            def shared_down(n, f, tiles=()):
                pe.wait_ge(s_h, n * NF + (f + 1))
                if f == 0:
                    wait(pe, s_add, n * 4)
                for c in range(4):
                    last = pe.matmul(ps[:, 4 + c, 0:D], h_buf[n][:, f % 2, P * c:P * (c + 1)], wd_sb[:, f, :],
                                     start=f == 0, stop=f == NF - 1)
                    if c < 3:
                        hidden_max(tiles, c)
                last.then_inc(s_hused, 1)

            def shared_up(n, f, w, bank, tiles=()):
                for k in range(KD):
                    last = pe.matmul(ps[:, bank, :], w[:, k, P * f:P * (f + 1)], xnT[:, k, 512 * n:512 * (n + 1)],
                                     start=k == 0, stop=k == KD - 1)
                    if k < KD - 1:
                        hidden_max(tiles, k)
                last.then_inc(s_up, 1)
                hidden_max(tiles, KD - 1)

            def hidden_max(tiles, n):
                if n < len(tiles):
                    v = tiles[n]
                    pe.wait_ge(ranks_copied, 1)
                    scores_for_max(v // 16, v // 16, 0, v % 16, 2 + v % 2)

            def scores_for_max(i, s, blk, u, bank=None):
                if u == 0:
                    pe.wait_ge(stack_loaded[s], blk * 32 + 32)
                if bank is not None:
                    wait(pe, max_done, i * 16 + (u - 1))
                else:
                    bank = u % 4
                    if isinstance(i, int) and i == 2 and u < 4:
                        pe.wait_ge(mem_used, NT // 2 - 1 + bank // 2)
                    wait(pe, max_done, i * 16 + (u - 3))
                g, st = divmod(u, ST)
                pe.matmul(ps[:, bank, :], q_st[s][0:R, g, P * st:P * (st + 1)], k_st[s][0:R, :],
                          start=True, stop=True).then_inc(a_ready, 1)

            def shared_group(n):
                for f in range(NF):
                    tiles = HIDDEN.get(f, ()) if n == 1 else ()
                    if n == 0:
                        wait(pe, s_h, max(f - 1, 0))
                        banks = f % 2, 2 + f % 2
                    else:
                        pe.wait_ge(s_h, n * NF + f)
                        banks = 0, 1
                    shared_up(n, f, wg_sb, banks[0], tiles[0:2])
                    shared_up(n, f, wu_sb, banks[1], tiles[2:4])
                    if f > 0:
                        shared_down(n, f - 1, tiles[4:])
                    elif n > 0:
                        shared_down(n - 1, NF - 1)

            pe.wait_ge(shw_loaded, 48)
            pe.wait_ge(v_copied, 2)
            pe.wait_ge(logits_copied, 1)
            pe.wait_ge(qk_copied, 12)
            shared_group(0)
            pe.wait_ge(onehot_ready, 1)
            pe.wait_ge(s_h, NF)
            W = TOPK * NT
            flags = onehot[:, :, :].rearrange("p w e -> p (w e)")
            pe.matmul(ps[:, 3, 0:W * E], before[:, :], flags, start=True, stop=True)
            pe.matmul(ps[:, 3, W * E:2 * W * E], ones[:, 0:P], flags, start=True, stop=True)\
              .then_inc(ranks_in_psum, 1)
            shared_group(1)
            def bank_free(i, turn, outputs=0):
                back = turn - 3
                if back < 0:
                    back, i = back + TURNS, i - 1
                if back == MAX_AT:
                    wait(pe, negm_ready, i + 2)
                elif back == OUT_AT:
                    wait(pe, oT_copied, outputs)
                else:
                    v = back - (back > MAX_AT) - (back > OUT_AT)
                    wait(pe, probs_ready, i * 16 + (v + 1))

            def transpose_max(i, s):
                pe.wait_ge(max_done, i * 16 + 16)
                bank_free(i - 1, MAX_AT)
                pe.transpose(ps[0:16, RING[MAX_AT % 3], 0:P], smax[:, s % 2, :], ident[:, :])\
                  .then_inc(maxT_in_psum, 1)

            shared_down(1, NF - 1)
            pe.wait_ge(mem_loaded, 64)
            pe.wait_ge(sigma_ready, KD)
            pe.wait_ge(s_h, 2 * NF)
            for c in range(NT):
                if c == 2:
                    pe.wait_ge(max_done, 32)
                if c == 4:
                    pe.wait_ge(s_add, 2 * 4)
                    transpose_max(0, 0)
                wait(pe, mem_used, c // 2 - 1)
                for m in range(KD):
                    last = pe.matmul(ps[:, c % 4, 2 * MEMW * m:2 * MEMW * (m + 1)], qf[:, m, P * c:P * (c + 1)],
                                     mem_w[:, :], start=True, stop=True)
                if c % 2:
                    last.then_inc(mem_in_psum, 1)

            pe.wait_ge(ones_rows, 64)

            def transpose_o(pair, a):
                pe.wait_ge(o_copied, pair + 1)
                if isinstance(pair, int) and pair == PAIRS - 1:
                    pe.wait_ge(probs_ready, STEPS * 16)
                else:
                    bank_free(pair * 2 + 2, OUT_AT)
                for st in range(ST):
                    last = pe.transpose(ps[:, RING[OUT_AT % 3], P * st:P * (st + 1)],
                                        o_sb[:, a, P * st:P * (st + 1)], ident[:, :])
                last.then_inc(oT_in_psum, 1)

            def weighted_values(i, s, t, pair=0):
                pe.wait_ge(probs_ready, i * 16 + 4 * (t + 1))
                if t == 0:
                    pe.wait_ge(v_head_ready, i + 1)
                    if s % 2 == 0:
                        wait(pe, o_copied, pair)
                for g in range(G):
                    last = pe.matmul(ps[32 * g:32 * (g + 1), 6, :], v_head[:, s % 2, t, :], probs[:, t % 2, g, :],
                                     start=s % 2 == 0 and t == 0, stop=s % 2 == 1 and t == ST - 1)
                last.then_inc(pv_done, 1)

            def transpose_x(j, pair, a):
                pe.wait_ge(ex_loaded[a], pair * 16 + 16)
                wait(pe, exT_ready, j)
                for k in range(KD):
                    last = pe.transpose(ps[:, 2, P * k:P * (k + 1)], e_x[:, a, P * k:P * (k + 1)], ident[:, :])
                last.then_inc(exT_in_psum, 1)

            def up(j, a, halves=(0, 1)):
                e = pe.value_load(expert[0:1, bass.ds(j, 1)], min_val=0, max_val=E - 1)
                pe.wait_ge(exT_ready, j + 1)
                wait(pe, h_ready, j - 1)
                for n in halves:
                    for k in range(KD):
                        w = w1_sb[:, bass.ds(e, 1), k, F * n:F * (n + 1)].rearrange("p o n -> p (o n)")
                        last = pe.matmul(ps[:, 4 * a + n, :], e_xT[:, a, k, :], w, start=k == 0, stop=k == KD - 1)
                    last.then_inc(up_done, 1)

            def step(blk, s, first=False, ahead=True, last=False):
                i = blk * 4 + s
                pair = blk * 2 + s // 2
                pe.wait_ge(m_loaded[s % 2], blk * 96 + 48 * (s // 2 + 1))
                for t in range(ST):
                    for g in range(G):
                        u = G * t + g
                        if not (last and turn_of(u) - 3 == MAX_AT):
                            bank_free(i, turn_of(u), pair if s % 2 == 0 else 0)
                        pe.matmul(ps[:, RING[turn_of(u) % 3], :], k_st[s][0:RM, P * t:P * (t + 1)],
                                  q_st[s][0:RM, g, :], start=True, stop=True).then_inc(scores_ready, 1)
                        if ahead:
                            scores_for_max(i + 2, (s + 2) % 4, blk + (s + 2) // 4, u)
                    if t == MAX_AT // G - 1 and not last:
                        transpose_max(i + 1, s + 1)
                    if t == OUT_AT // G - 1 and s % 2 == 0 and not first:
                        transpose_o(pair - 1, (s // 2 + 1) % 2)
                    if t > 0:
                        weighted_values(i, s, t - 1, pair)
                    elif not first:
                        weighted_values(i - 1, s + 3, ST - 1)
                    if last and t == 0:
                        pe.wait_ge(experts_known, 1)
                        pe.wait_ge(w12_loaded, 16 * 2 * E)
                        transpose_x(0, 0, 0)
                    if last and t in (1, 2):
                        up(0, 0, (t - 1,))
                    if last and t == 3:
                        transpose_x(1, 0, 1)

            for i in range(4):
                step(0, i, first=i == 0)
            with pe.Fori(1, NLOOP - 1) as blk:
                for s in range(4):
                    step(blk, s)
            for i in range(STEPS - 4, STEPS):
                step(NLOOP - 1, i % 4, ahead=i + 2 < STEPS, last=i == STEPS - 1)
            weighted_values(STEPS - 1, STEPS - 1, ST - 1)
            def transpose_h(j, a):
                pe.wait_ge(h_ready, j + 1)
                wait(pe, hT_ready, j)
                for k in range(F // P):
                    last = pe.transpose(ps[:, 3, P * k:P * (k + 1)], e_h[:, a, P * k:P * (k + 1)], ident[:, :])
                last.then_inc(hT_in_psum, 1)

            def down(j, a):
                e = pe.value_load(expert[0:1, bass.ds(j, 1)], min_val=0, max_val=E - 1)
                pe.wait_ge(hT_ready, j + 1)
                wait(pe, y_ready, j - 1)
                for k in range(F // P):
                    w = w2_sb[:, bass.ds(e, 1), k, :].rearrange("p o n -> p (o n)")
                    last = pe.matmul(ps[:, 6 + a, 0:D], e_hT[:, a, k, :], w, start=k == 0, stop=k == F // P - 1)
                last.then_inc(y_in_psum, 1)

            def tile(j, pair, a):
                if live(j) and not (isinstance(j, int) and j == 0):
                    up(j, a)
                if live(j - 1):
                    transpose_h(j - 1, 1 - a)
                if live(j + 1) and not (isinstance(j, int) and j == 0):
                    transpose_x(j + 1, pair + a, 1 - a)
                if live(j - 2):
                    down(j - 2, a)

            pe.wait_ge(probs_ready, 16 * STEPS)
            transpose_o(PAIRS - 1, 1)
            pe.wait_ge(oT_copied, PAIRS)
            over_tiles(pe, tile)

            def split_up(m):
                n, f = m // NF, m % NF
                tokens = slice(512 * n, 512 * (n + 1))
                wait(pe, s_h, FIRST + m - 1 if m > 1 else 0)
                for w in range(2):
                    for count, (weights, xs, w_sem, x_sem) in enumerate((
                            (w_hi[f], x_hi, w_hi_ready, x_hi_ready), (w_hi[f], x_lo, w_hi_ready, x_lo_ready),
                            (w_lo[f], x_hi, w_lo_ready, x_hi_ready))):
                        pe.wait_ge(w_sem, f + 1)
                        pe.wait_ge(x_sem, n + 1)
                        for k in range(KD):
                            part = P * (KD * w + k)
                            last = pe.matmul(ps[:, 2 * w + m % 2, :], weights[:, part:part + P], xs[:, k, tokens],
                                             start=count == 0 and k == 0, stop=count == 2 and k == KD - 1)
                    last.then_inc(s_up, 1)

            def split_down(m):
                f = m % NF
                pe.wait_ge(h_lo_ready, m + 1)
                if m == 0:
                    pe.wait_ge(y_ready, TILES)
                if f == 0:
                    pe.wait_ge(s_add, 4 * (2 + m // NF))
                for c in range(4):
                    part = slice(P * c, P * (c + 1))
                    for count, (h, w) in enumerate(((h_hi[m % 3], w_hi[f]), (h_hi[m % 3], w_lo[f]),
                                                    (h_lo[m % 3], w_hi[f]))):
                        last = pe.matmul(ps[:, 4 + c, 0:D], h[:, part], w[:, 512:768],
                                         start=f == 0 and count == 0, stop=f == NF - 1 and count == 2)
                last.then_inc(s_hused, 1)

            for m in range(LAST):
                split_up(m)
                if m >= 2:
                    split_down(m - 2)
            split_down(LAST - 2)
            split_down(LAST - 1)


def kernel(L0_attn_x, L0_attn_Wq, L0_attn_Wk, L0_attn_Wv, L0_attn_memory, L0_attn_memory_norm, L0_attn_memory_weight,
           L0_ffn_router_w, L0_ffn_w1, L0_ffn_w2, L0_ffn_w_gate, L0_ffn_w_up, L0_ffn_w_down):
    import concourse.bacc as bacc
    from concourse.bass_utils import run_bass_kernel_spmd

    arrays = {
        "x": L0_attn_x, "wqT": np.asarray(L0_attn_Wq).T, "wkT": np.asarray(L0_attn_Wk).T,
        "wvT": np.asarray(L0_attn_Wv).T, "memory": L0_attn_memory, "memory_norm": L0_attn_memory_norm,
        "memory_weight": L0_attn_memory_weight, "router_w": L0_ffn_router_w, "w1": L0_ffn_w1, "w2": L0_ffn_w2,
        "w_gate": L0_ffn_w_gate, "w_up": L0_ffn_w_up, "w_down": L0_ffn_w_down,
    }
    arrays = {name: np.ascontiguousarray(a) for name, a in arrays.items()}
    nc = bacc.Bacc("TRN2", target_bir_lowering=False, num_devices=1)
    args = [nc.dram_tensor(name, a.shape, mybir.dt.from_np(a.dtype), kind="ExternalInput").ap()
            for name, a in arrays.items()]
    out = nc.dram_tensor("out", arrays["x"].shape, F32, kind="ExternalOutput").ap()
    build(nc, *args, out)
    result = run_bass_kernel_spmd(nc, [arrays], core_ids=[0])
    return result.results[0]["out"]
```
